# Optimizing a Trainium2 kernel written in Bass

```python
import numpy as np
import jax
import jax.numpy as jnp

def _softmax(x, axis=-1):
    return jax.nn.softmax(x, axis=axis)
def _gelu(x):
    return jax.nn.gelu(x, approximate=True)
def _silu(x):
    return jax.nn.silu(x)
def _sigmoid(x):
    return jax.nn.sigmoid(x)
def _layernorm(x, axis=-1, eps=1e-5):
    m = jnp.mean(x, axis=axis, keepdims=True)
    v = jnp.var(x, axis=axis, keepdims=True)
    return (x - m) / jnp.sqrt(v + eps)
def _scatter_add(tgt, idx, src, axis=0):
    return tgt.at[idx].add(src)
def _segment_sum(src, seg, n):
    return jax.ops.segment_sum(src, seg, n)

kernel_name = 'mk_adj_preln_d4_adj_128_61317d'

def setup_inputs(seed: int = 0):
    np.random.seed(seed)
    _w = jnp.asarray
    def _rec_inputs():
        import jax
        import jax.numpy as jnp
        _gk = jax.random.key(seed)
        x = -0.0005207 + 1.001 * jax.random.normal(jax.random.fold_in(_gk, 1), (16, 1024, 128), jnp.float32)
        _a = jax.random.bernoulli(jax.random.fold_in(_gk, 2), 0.03125, (1024, 1024))
        adj = _a.astype(jnp.int32)
        return x, adj
    x, adj = _rec_inputs()
    def _L0_gnn_setup():
        import jax, jax.numpy as jnp
        import numpy as np
        NEG_BIG = -9000000000000000.0
        LEAKY_SLOPE = 0.2
        key = jax.random.key(seed)
        k1, k2, k3, k4 = jax.random.split(key, 4)
        B, N, F_in, F_out = (8, 2048, 128, 128)
        h = jax.random.normal(k1, (B, N, F_in), dtype=jnp.float32)
        adj = jax.random.randint(k2, (N, N), 0, 2).astype(jnp.int32)
        W = jax.random.normal(k3, (F_in, F_out), dtype=jnp.float32) * 0.05
        a = jax.random.normal(k4, (2 * F_out,), dtype=jnp.float32) * 0.05
        return {'h': h, 'adj': adj, 'W': W, 'a': a}
    _L0_gnn_all = _L0_gnn_setup()
    _L0_gnn_in = {k: v for k, v in _L0_gnn_all.items() if k in ('W', 'a', )}
    del _L0_gnn_all

    def _L1_gnn_setup():
        import jax, jax.numpy as jnp
        import numpy as np
        NEG_BIG = -9000000000000000.0
        ALPHA = 0.2
        key = jax.random.key(seed)
        k = jax.random.split(key, 6)
        B, N, D, H = (1, 4096, 128, 8)
        x = jax.random.normal(k[0], (B, N, D), dtype=jnp.float32)
        adj = jax.random.randint(k[1], (N, N), 0, 2, dtype=jnp.int32)
        W = jax.random.normal(k[2], (H, D, D), dtype=jnp.float32) * 0.1
        a = jax.random.normal(k[3], (H, 2 * D, 1), dtype=jnp.float32) * 0.1
        avg_w = jax.random.normal(k[4], (1, H), dtype=jnp.float32) * 0.3
        avg_b = jax.random.normal(k[5], (1,), dtype=jnp.float32) * 0.1
        return {'x': x, 'adj': adj, 'W': W, 'a': a, 'avg_w': avg_w, 'avg_b': avg_b}
    _L1_gnn_all = _L1_gnn_setup()
    _L1_gnn_in = {k: v for k, v in _L1_gnn_all.items() if k in ('W', 'a', 'avg_w', 'avg_b', )}
    del _L1_gnn_all

    def _L2_gnn_setup():
        import jax, jax.numpy as jnp
        import numpy as np
        NEG_BIG = -9000000000000000.0
        key = jax.random.key(seed)
        k1, k2, k3, k4 = jax.random.split(key, 4)
        B, N, C, D = (8, 2048, 128, 128)
        x = jax.random.normal(k1, (B, N, C), dtype=jnp.float32)
        adj = jax.random.randint(k2, (N, N), 0, 2, dtype=jnp.int32)
        W = jax.random.normal(k3, (D, C), dtype=jnp.float32) * (1.0 / np.sqrt(C))
        a = jax.random.normal(k4, (1, 2 * D), dtype=jnp.float32) * (1.0 / np.sqrt(2 * D))
        return {'x': x, 'adj': adj, 'W': W, 'a': a}
    _L2_gnn_all = _L2_gnn_setup()
    _L2_gnn_in = {k: v for k, v in _L2_gnn_all.items() if k in ('W', 'a', )}
    del _L2_gnn_all

    def _L3_gnn_setup():
        import jax, jax.numpy as jnp
        import numpy as np
        B, N, F_IN, F_OUT = (8, 2048, 128, 128)
        key = jax.random.key(seed)
        k1, k2, k3, k4 = jax.random.split(key, 4)
        x = jax.random.normal(k1, (B, N, F_IN), dtype=jnp.float32)
        adj = jax.random.randint(k2, (N, N), 0, 2, dtype=jnp.int32)
        W = jax.random.normal(k3, (F_OUT, F_IN), dtype=jnp.float32) * 0.05
        a = jax.random.normal(k4, (2 * F_OUT, 1), dtype=jnp.float32) * 0.05
        return {'x': x, 'adj': adj, 'W': W, 'a': a}
    _L3_gnn_all = _L3_gnn_setup()
    _L3_gnn_in = {k: v for k, v in _L3_gnn_all.items() if k in ('W', 'a', )}
    del _L3_gnn_all

    return {
        "x": x,
        "adj": adj,
        "L0_gnn_W": _L0_gnn_in["W"],
        "L0_gnn_a": _L0_gnn_in["a"],
        "L1_gnn_W": _L1_gnn_in["W"],
        "L1_gnn_a": _L1_gnn_in["a"],
        "L1_gnn_avg_w": _L1_gnn_in["avg_w"],
        "L1_gnn_avg_b": _L1_gnn_in["avg_b"],
        "L2_gnn_W": _L2_gnn_in["W"],
        "L2_gnn_a": _L2_gnn_in["a"],
        "L3_gnn_W": _L3_gnn_in["W"],
        "L3_gnn_a": _L3_gnn_in["a"],
    }

def reference(x, adj, L0_gnn_W, L0_gnn_a, L1_gnn_W, L1_gnn_a, L1_gnn_avg_w, L1_gnn_avg_b, L2_gnn_W, L2_gnn_a, L3_gnn_W, L3_gnn_a):
    import jax
    import jax.numpy as jnp
    def _L0_gnn_ref(h, adj, W, a):
        import jax, jax.numpy as jnp
        import numpy as np
        NEG_BIG = -9000000000000000.0
        LEAKY_SLOPE = 0.2
        Wh = jnp.einsum('bnf,fo->bno', h, W)
        F_out = Wh.shape[-1]
        a_src, a_dst = (a[:F_out], a[F_out:])
        s_src = jnp.einsum('bnf,f->bn', Wh, a_src)
        s_dst = jnp.einsum('bnf,f->bn', Wh, a_dst)
        e = jax.nn.leaky_relu(s_src[:, :, None] + s_dst[:, None, :], negative_slope=LEAKY_SLOPE)
        masked = jnp.where(adj[None, :, :] > 0, e, NEG_BIG)
        attention = jax.nn.softmax(masked, axis=-1)
        h_prime = jnp.einsum('bij,bjf->bif', attention, Wh)
        return h_prime

    def _L1_gnn_ref(x, adj, W, a, avg_w, avg_b):
        import jax, jax.numpy as jnp
        import numpy as np
        NEG_BIG = -9000000000000000.0
        ALPHA = 0.2
        D = W.shape[-1]
        hW = jnp.einsum('bnd,hde->hbne', x, W)
        a1 = a[:, :D, 0]
        a2 = a[:, D:, 0]
        s1 = jnp.einsum('hbnd,hd->hbn', hW, a1)
        s2 = jnp.einsum('hbnd,hd->hbn', hW, a2)
        e = s1[..., :, None] + s2[..., None, :]
        e = jax.nn.leaky_relu(e, ALPHA)
        e = jax.nn.softmax(e, axis=-1)
        att = jnp.where(adj > 0, e, jnp.float32(NEG_BIG))
        out_h = jax.nn.sigmoid(jnp.einsum('hbnm,hbmd->hbnd', att, hW))
        out = jnp.einsum('hbnd,h->bnd', out_h, avg_w[0]) + avg_b[0]
        return out

    def _L2_gnn_ref(x, adj, W, a):
        import jax, jax.numpy as jnp
        import numpy as np
        NEG_BIG = -9000000000000000.0
        Wh = jnp.einsum('bnc,dc->bnd', x, W)
        D = Wh.shape[-1]
        a1, a2 = (a[0, :D], a[0, D:])
        f1 = Wh @ a1
        f2 = Wh @ a2
        e = jax.nn.leaky_relu(f1[:, :, None] + f2[:, None, :], negative_slope=0.2)
        e = jnp.where(adj[None] > 0, e, NEG_BIG)
        attention = jax.nn.softmax(e, axis=-1)
        h_prime = jnp.einsum('bij,bjd->bid', attention, Wh)
        return jax.nn.elu(h_prime)

    def _L3_gnn_ref(x, adj, W, a):
        import jax, jax.numpy as jnp
        import numpy as np
        B, N, F_IN, F_OUT = (8, 2048, 128, 128)
        h = jnp.einsum('bni,oi->bno', x, W)
        fo = W.shape[0]
        a_src = a[:fo, 0]
        a_dst = a[fo:, 0]
        s = jnp.einsum('bnf,f->bn', h, a_src)
        d = jnp.einsum('bnf,f->bn', h, a_dst)
        e = s[:, :, None] + d[:, None, :]
        e = jnp.where(e > 0, e, 0.2 * e)
        e = jnp.where(adj[None, :, :] == 0, jnp.float32(-1000000000.0), e)
        attention = jax.nn.softmax(e, axis=-1)
        return jnp.einsum('bij,bjf->bif', attention, h)

    h = jnp.maximum(_layernorm(x, axis=-1), 0.0)
    x = x + _L0_gnn_ref(h, adj, L0_gnn_W, L0_gnn_a)
    h = jnp.maximum(_layernorm(x, axis=-1), 0.0)
    x = x + _L1_gnn_ref(h, adj, L1_gnn_W, L1_gnn_a, L1_gnn_avg_w, L1_gnn_avg_b)
    h = jnp.maximum(_layernorm(x, axis=-1), 0.0)
    x = x + _L2_gnn_ref(h, adj, L2_gnn_W, L2_gnn_a)
    h = jnp.maximum(_layernorm(x, axis=-1), 0.0)
    x = x + _L3_gnn_ref(h, adj, L3_gnn_W, L3_gnn_a)
    return x


_drawn_inputs = setup_inputs


def setup_inputs(seed=0):
    import zlib

    import numpy as np

    out = dict(_drawn_inputs(seed))
    spreads = {}
    factors = {'L3_gnn_a': 8.0}
    for name, (base, spread) in spreads.items():
        noise = np.random.default_rng([zlib.crc32(name.encode()), seed]).standard_normal(out[name].shape)
        drawn = base * np.exp(spread * noise) if base else spread * noise
        out[name] = jnp.asarray(drawn.astype(out[name].dtype))
    for name, factor in factors.items():
        out[name] = (out[name] * factor).astype(out[name].dtype)
    return out
```

```python
from contextlib import ExitStack

import concourse.bass as bass
from concourse import mybir

FP32 = mybir.dt.float32
BF16 = mybir.dt.bfloat16
INT32 = mybir.dt.int32
UINT8 = mybir.dt.uint8
ALU = mybir.AluOpType
ACT = mybir.ActivationFunctionType
AX_X = mybir.AxisListType.X
REDUCE_MAX = bass.bass_isa.ReduceOp.max

B = 16
N = 1024
D = 128
P = 128
T = N // P
H = 8
HALF = 512
RING = 4
EPS = 1e-5
SLOPE = 0.2
NEG_BIG = -9.0e15

RISE = 1.0 - SLOPE
SHIFT = 20.0
T_MAX = 93.0
Q_MAX = 105.0

W_ROW = {0: 0, 2: 1, 3: 2}
W_HEADS = 3


def wait_for(eng, sem, value):
    if isinstance(value, int) and value <= 0:
        return
    eng.wait_ge(sem, value)


def wait_alone(eng, passed, sem, value):
    wait_for(eng, sem, value)
    if not isinstance(value, int):
        eng.sem_inc(passed, 1)


class Shared:
    pass


def setup(nc, g, ins):
    x_h, adj_h, w_in_h, w_out_h, a_h, avg_w_h, avg_b_h = ins
    with ExitStack() as ctx:
        def sb(name, shape, dt):
            return ctx.enter_context(nc.sbuf_tensor(name, shape, dt))

        def sem(name):
            return ctx.enter_context(nc.semaphore(name))

        adj_rows = sb("adj_rows", [P, 4, N], INT32)
        mask_rows = sb("mask_rows", [P, 2, 2, N], BF16)
        w_out = sb("w_out", [P, W_HEADS + H, D], FP32)
        a_cols = sb("a_cols", [P, W_HEADS + H, 2], FP32)
        row_max = sb("row_max", [P, 2, T], FP32)
        ident_bf = sb("ident_bf", [P, P], BF16)
        mask_ps = ctx.enter_context(nc.psum_tensor("mask_ps", [P, 4, N], BF16))
        wa_ps = ctx.enter_context(nc.psum_tensor("wa_ps", [P, HALF], FP32))

        adj_in = [sem(f"adj_in{i}") for i in range(4)]
        w_loaded, x_loaded = sem("w_loaded"), sem("x_loaded")
        ident_zero, ident_made, sel_zero, sel_made = sem("ident_zero"), sem("ident_made"), sem("sel_zero"), sem("sel_made")
        masks_made, masks_turned, mask1_copied, mask3_copied = (
            sem("masks_made"), sem("masks_turned"), sem("mask1_copied"), sem("mask3_copied"))
        wa_done, wa_copied, row_max_done, ident_bf_made = sem("wa_done"), sem("wa_copied"), sem("row_max_done"), sem("ident_bf_made")

        block = ctx.enter_context(nc.Block())

        @block.sync
        def _(sp):
            for it in range(T):
                if it >= 4:
                    sp.wait_ge(masks_made, it - 3)
                sp.dma_start(adj_rows[:, it % 4, :], adj_h[it * P:(it + 1) * P, :]).then_inc(adj_in[it % 4], 16)
            sp.wait_ge(x_loaded, 64)

        @block.scalar
        def _(act):
            act.dma_start(w_out[:], w_out_h).then_inc(w_loaded, 16)
            act.dma_start(a_cols[:], a_h).then_inc(w_loaded, 16)
            act.dma_start(g.w_in[:], w_in_h).then_inc(w_loaded, 16)
            act.dma_start(g.avg_w[:], avg_w_h).then_inc(w_loaded, 16)
            act.dma_start(g.avg_b[:], avg_b_h).then_inc(w_loaded, 16)
            for c in range(4):
                act.dma_start(g.x[:, 4 * c:4 * c + 4, :, :],
                              x_h[4 * c:4 * c + 4].rearrange("b (t p) d -> p b t d", p=P)).then_inc(x_loaded, 16)
            for it in range(T):
                act.wait_ge(masks_turned, 2 * it + 1)
                nc.scalar.activation(g.mask_gt[:, :, it * P:(it + 1) * P],
                                     mask_ps[:, (2 * it) % 4, :].rearrange("p (t i) -> p t i", t=T),
                                     ACT.Copy).then_inc(mask1_copied, 1)

        @block.gpsimd
        def _(pool):
            nc.gpsimd.memset(g.ident[:], 0.0).then_inc(ident_zero, 1)
            pool.wait_ge(ident_zero, 1)
            nc.gpsimd.affine_select(out=g.ident[:], in_=g.ident[:], compare_op=ALU.not_equal, fill=1.0, base=0,
                                    pattern=[[-1, P]], channel_multiplier=1).then_inc(ident_made, 1)
            nc.gpsimd.memset(g.sel[:], 0.0).then_inc(sel_zero, 1)
            pool.wait_ge(sel_zero, 1)
            for part in range(3):
                nc.gpsimd.affine_select(out=g.sel[:], in_=g.sel[:], compare_op=ALU.not_equal, fill=1.0,
                                        base=-32 * part, pattern=[[-1, H], [0, P]],
                                        channel_multiplier=1).then_inc(sel_made, 1)
                pool.wait_ge(sel_made, part + 1)
            nc.gpsimd.memset(g.minus_half[:], -0.5)
            nc.gpsimd.memset(g.bias_up[:], SHIFT)
            nc.gpsimd.memset(g.bias_down[:], -SHIFT)
            nc.gpsimd.memset(g.bias_r[:], RISE * T_MAX - SHIFT)

        def copy_mask3(dve, it):
            dve.wait_ge(masks_turned, 2 * it + 2)
            nc.vector.tensor_copy(g.mask_ne[:, :, it * P:(it + 1) * P],
                                  mask_ps[:, (2 * it + 1) % 4, :].rearrange("p (t i) -> p t i", t=T)
                                  ).then_inc(mask3_copied, 1)

        @block.vector
        def _(dve):
            dve.wait_ge(ident_made, 1)
            nc.vector.tensor_copy(ident_bf[:], g.ident[:]).then_inc(ident_bf_made, 1)
            for it in range(T):
                dve.wait_ge(adj_in[it % 4], 16 * (it // 4 + 1))
                if it >= 2:
                    dve.wait_ge(masks_turned, 2 * (it - 1))
                rows = adj_rows[:, it % 4, :]
                nc.vector.tensor_reduce(row_max[:, 0, it:it + 1], rows, AX_X, ALU.max)
                nc.vector.tensor_reduce(row_max[:, 1, it:it + 1], rows, AX_X, ALU.max,
                                        apply_absolute_value=True).then_inc(row_max_done, 1)
                nc.vector.tensor_scalar(mask_rows[:, it % 2, 0, :], rows, 0.0, None, ALU.is_gt)
                nc.vector.tensor_scalar(mask_rows[:, it % 2, 1, :], rows, 0.0, None,
                                        ALU.not_equal).then_inc(masks_made, 1)
                if it >= 1:
                    copy_mask3(dve, it - 1)
            copy_mask3(dve, T - 1)
            dve.wait_ge(row_max_done, T)
            nc.vector.tensor_scalar(g.empty_gt[:], row_max[:, 0, :], 0.0, None, ALU.is_le)
            nc.vector.tensor_scalar(g.empty_ne[:], row_max[:, 1, :], 0.0, None, ALU.is_le)
            dve.wait_ge(wa_done, 1)
            nc.vector.tensor_copy(g.wa[:], wa_ps[:, 0:2 * (W_HEADS + H)].rearrange("p (l t) -> p l t", t=2))
            nc.vector.tensor_copy(g.wa_heads[:], wa_ps[:, 2 * W_HEADS:2 * (W_HEADS + H)]
                                  .rearrange("p (h t) -> p t h", t=2)).then_inc(wa_copied, 1)
            dve.wait_ge(wa_copied, 1)
            dve.wait_ge(w_loaded, 80)
            nc.vector.tensor_scalar(g.half_w[:], g.avg_w[:], 0.5, None, ALU.mult).then_inc(wa_copied, 1)
            dve.wait_ge(wa_copied, 2)
            nc.vector.tensor_reduce(g.half_sum[:], g.half_w[:], AX_X, ALU.add).then_inc(wa_copied, 1)
            dve.wait_ge(wa_copied, 3)
            nc.vector.tensor_tensor(g.base1[:], g.half_sum[:], g.avg_b[:], ALU.add)

        @block.tensor
        def _(pe):
            pe.wait_ge(ident_bf_made, 1)
            for it in range(T):
                pe.wait_ge(masks_made, it + 1)
                for kind in range(2):
                    if it >= 2:
                        pe.wait_ge((mask1_copied, mask3_copied)[kind], it - 1)
                    for jt in range(T):
                        last = nc.tensor.transpose(mask_ps[:, (2 * it + kind) % 4, jt * P:(jt + 1) * P],
                                                   mask_rows[:, it % 2, kind, jt * P:(jt + 1) * P], ident_bf[:])
                    last.then_inc(masks_turned, 1)
            pe.wait_ge(w_loaded, 80)
            for row in range(W_HEADS + H):
                last = nc.tensor.matmul(wa_ps[:, 2 * row:2 * row + 2], w_out[:, row, :], a_cols[:, row, :],
                                        start=True, stop=True)
            last.then_inc(wa_done, 1)


def masked_semaphores(nc, ctx):
    names = ["stats", "moments", "var_ready", "rstd", "normed", "turned", "h_ready", "cols_done", "cols_read", "dmax_ready",
             "drop_ready", "args_ready", "src_done", "src_read", "u_ready", "q_ready", "r_ready", "v_done", "v_ready",
             "tile_ready", "tile_used", "empty_ready", "addend_ready", "den_ready", "recip_ready", "acc_read",
             "low_ready", "elu_exp", "elu_less", "x_done"]
    return {n: ctx.enter_context(nc.semaphore("m_" + n)) for n in names}


def masked_layer(nc, g, s, layer, order, out_h):
    mask = g.mask_ne if layer == 3 else g.mask_gt
    empty = g.empty_ne if layer == 3 else g.empty_gt
    elu = layer == 2
    w = g.w_in[:, W_ROW[layer], :]
    wa = g.wa[:, W_ROW[layer], :]
    wa_rep = wa[:, 0:1].to_broadcast([P, P])
    done = B * order
    x_batches = 0 if layer == 0 else B
    V1 = D + 1

    with ExitStack() as ctx:
        def sb(name, shape, dt=FP32):
            return ctx.enter_context(nc.sbuf_tensor(f"{name}_l{layer}", shape, dt))

        stats, mom = sb("stats", [P, T, 6]), sb("mom", [P, T, 2])
        var_eps, rstd = sb("var_eps", [P, T]), sb("rstd", [P, T])
        hn = sb("hn", [P, T, D])
        h_t = sb("h_t", [P, 2, N])
        h_sum = sb("h_sum", [P, 2])
        cols = sb("cols", [P, 2, T, 2])
        mean_v = sb("mean_v", [P, 2, D])
        dmax1 = sb("dmax1", [P, 1])
        dmax = sb("dmax", [P, 2])
        clamp = sb("clamp", [P, 2])
        drop = sb("drop", [P, 2, T])
        rise = sb("rise", [P, 2, T])
        q = sb("q", [P, 2, T])
        r_row = sb("r_row", [P, 2, N])
        v = sb("v", [P, 2, T, V1])
        tiles = sb("tiles", [P, RING, N])
        spread = sb("spread", [P, T, D])
        addend = sb("addend", [P, 2, T, D])
        den, recip = sb("den", [P, T]), sb("recip", [P, T])
        if elu:
            y, low, ex = sb("y", [P, T, D]), sb("low", [P, T, D]), sb("ex", [P, T, D])
        ps = ctx.enter_context(nc.psum_tensor(f"ps_l{layer}", [P, 8, HALF], FP32))
        aux = ps[:, 6:8, :]
        out_done = ctx.enter_context(nc.semaphore(f"out_done{layer}"))

        def acc(par, it, lo, hi):
            at = (it % 3) * V1
            return ps[:, 3 * par + it // 3, at + lo:at + hi]

        block = ctx.enter_context(nc.Block())

        @block.vector
        def _(dve):
            def norm(b, par):
                n = done + b
                wait_for(dve, s["turned"], n)
                for it in range(T):
                    last = nc.vector.bn_stats(stats[:, it, :], g.x[:, b, it, :])
                last.then_inc(s["stats"], 1)
                wait_alone(dve, g.dve_passed, s["stats"], n + 1)
                for it in range(T):
                    last = nc.vector.bn_aggr(mom[:, it, :], stats[:, it, :])
                last.then_inc(s["moments"], 1)
                dve.wait_ge(s["moments"], n + 1)
                nc.vector.tensor_scalar(var_eps[:], mom[:, :, 1], EPS, None, ALU.add).then_inc(s["var_ready"], 1)
                dve.wait_ge(s["rstd"], n + 1)
                for it in range(T):
                    last = nc.vector.tensor_scalar(hn[:, it, :], g.x[:, b, it, :], mom[:, it, 0:1],
                                                   rstd[:, it:it + 1], ALU.subtract, ALU.mult)
                last.then_inc(s["normed"], 1)

            def read_cols(b, par):
                n = done + b
                dve.wait_ge(s["cols_done"], n + 1)
                wait_for(dve, s["empty_ready"], n - 1)
                ps_cols = aux[:, 0, 0:2 * T].rearrange("p (t c) -> p t c", c=2)
                nc.vector.tensor_reduce(dmax1[:], aux[:, 0, 0:2 * T].rearrange("p (t c) -> p c t", c=2)[:, 1, :],
                                        AX_X, ALU.max)
                nc.vector.tensor_copy(cols[:, par], ps_cols)
                nc.vector.tensor_scalar(mean_v[:, par, :], aux[:, 1, 0:D], 1.0 / N, None,
                                        ALU.mult).then_inc(s["cols_read"], 1)

            def exponents(b, par):
                n = done + b
                dve.wait_ge(s["dmax_ready"], n + 1)
                wait_for(dve, s["q_ready"], n - 1)
                wait_for(dve, s["src_read"], n - 1)
                nc.vector.tensor_scalar(clamp[:, par:par + 1], dmax[:, par:par + 1], -1.0, T_MAX, ALU.mult, ALU.add)
                nc.vector.tensor_scalar(drop[:, par, :], cols[:, par, :, 1], dmax[:, par:par + 1], None,
                                        ALU.subtract).then_inc(s["drop_ready"], 1)
                dve.wait_ge(s["drop_ready"], n + 1)
                nc.vector.tensor_scalar(rise[:, par, :], drop[:, par, :], -RISE, Q_MAX, ALU.mult,
                                        ALU.min).then_inc(s["args_ready"], 1)

            def tile(b, par, k):
                n = done + b
                if k == 0:
                    dve.wait_ge(s["q_ready"], n + 1)
                    dve.wait_ge(s["r_ready"], n + 1)
                wait_for(dve, s["tile_used"], T * n + k - RING + 1)
                nc.vector.scalar_tensor_tensor(tiles[:, k % RING, :], r_row[:, par, :], q[:, par, k:k + 1],
                                               mask[:, k, :], ALU.max, ALU.mult).then_inc(s["tile_ready"], 1)

            def finish(b, par):
                n = done + b
                dve.wait_ge(s["tile_used"], T * (n + 1))
                for bank in range(3):
                    lo, hi = 3 * bank, min(3 * bank + 3, T)
                    sums = ps[:, 3 * par + bank, 0:(hi - lo) * V1].rearrange("p (t c) -> p t c", c=V1)[:, :, D]
                    last = nc.vector.tensor_tensor(den[:, lo:hi], sums, empty[:, lo:hi], ALU.add)
                last.then_inc(s["den_ready"], 1)
                dve.wait_ge(s["den_ready"], n + 1)
                nc.vector.reciprocal(recip[:], den[:]).then_inc(s["recip_ready"], 1)
                dve.wait_ge(s["recip_ready"], n + 1)
                if elu:
                    dve.wait_ge(s["empty_ready"], n + 1)
                else:
                    dve.wait_ge(s["addend_ready"], x_batches + b + 1)
                for it in range(T):
                    dst = y[:, it, :] if elu else g.x[:, b, it, :]
                    last = nc.vector.scalar_tensor_tensor(dst, acc(par, it, 0, D), recip[:, it:it + 1],
                                                          addend[:, par, it, :], ALU.mult, ALU.add)
                last.then_inc(s["acc_read"], 1)
                if elu:
                    dve.wait_ge(s["acc_read"], n + 1)
                    wait_for(dve, s["elu_exp"], b)
                    nc.vector.tensor_scalar(low[:], y[:], 0.0, None, ALU.min)
                    nc.vector.scalar_tensor_tensor(g.x[:, b], y[:], 0.0, g.x[:, b], ALU.max,
                                                   ALU.add).then_inc(s["low_ready"], 1)

            def step(b, par, has_next=True, has_second=True, has_before=True):
                tile(b, par, 0)
                tile(b, par, 1)
                if has_next:
                    read_cols(b + 1, 1 - par)
                if has_second:
                    norm(b + 2, par)
                tile(b, par, 2)
                if has_next:
                    exponents(b + 1, 1 - par)
                tile(b, par, 3)
                if has_before:
                    finish(b - 1, 1 - par)
                for k in range(4, T):
                    tile(b, par, k)

            norm(0, 0)
            norm(1, 1)
            read_cols(0, 0)
            exponents(0, 0)
            step(0, 0, has_before=False)
            with dve.Fori(0, (B - 4) // 2) as j:
                step(2 * j + 1, 1)
                step(2 * j + 2, 0)
            step(B - 3, 1)
            step(B - 2, 0, has_second=False)
            step(B - 1, 1, has_next=False, has_second=False)
            finish(B - 1, 1)

        @block.scalar
        def _(act):
            def relu_h(b, par):
                n = done + b
                act.wait_ge(s["turned"], n + 1)
                wait_for(act, s["v_done"], n - 1)
                nc.scalar.activation(h_t[:, par, :].rearrange("p (a n) -> p a n", a=2), aux, ACT.Relu,
                                     accum_out=h_sum[:, par:par + 1]).then_inc(s["h_ready"], 1)

            def exps(b, par):
                n = done + b
                act.wait_ge(s["args_ready"], n + 1)
                act.wait_ge(s["src_done"], n + 1)
                wait_for(act, s["tile_used"], T * (n - 1))
                nc.scalar.activation(r_row[:, par, :].rearrange("p (a n) -> p a n", a=2), aux, ACT.Relu,
                                     bias=clamp[:, par:par + 1], scale=-1.0).then_inc(s["src_read"], 1)
                nc.scalar.activation(v[:, par, :, D], drop[:, par, :], ACT.Exp,
                                     bias=g.bias_up[:]).then_inc(s["u_ready"], 1)
                nc.scalar.activation(q[:, par, :], rise[:, par, :], ACT.Exp,
                                     bias=g.bias_down[:]).then_inc(s["q_ready"], 1)
                act.wait_ge(s["src_read"], n + 1)
                nc.scalar.activation(r_row[:, par, :], r_row[:, par, :], ACT.Exp, bias=g.bias_r[:],
                                     scale=-RISE).then_inc(s["r_ready"], 1)

            def values(b, par):
                n = done + b
                act.wait_ge(s["v_done"], n + 1)
                act.wait_ge(s["u_ready"], n + 1)
                for jt in range(T):
                    last = nc.scalar.activation(v[:, par, jt, 0:D], aux[:, jt // 4, (jt % 4) * D:(jt % 4 + 1) * D],
                                                ACT.Copy, scale=v[:, par, jt, D:V1])
                last.then_inc(s["v_ready"], 1)

            def elu_exp(b):
                act.wait_ge(s["low_ready"], b + 1)
                wait_for(act, s["x_done"], b)
                nc.scalar.activation(ex[:], low[:], ACT.Exp).then_inc(s["elu_exp"], 1)

            def step(b, par, has_next=True, has_second=True, has_before=True):
                if has_next:
                    exps(b + 1, 1 - par)
                if has_next:
                    values(b + 1, 1 - par)
                if has_second:
                    relu_h(b + 2, par)
                if elu and has_before:
                    elu_exp(b - 1)

            relu_h(0, 0)
            exps(0, 0)
            values(0, 0)
            relu_h(1, 1)
            step(0, 0, has_before=False)
            with act.Fori(0, (B - 4) // 2) as j:
                step(2 * j + 1, 1)
                step(2 * j + 2, 0)
            step(B - 3, 1)
            step(B - 2, 0, has_second=False)
            step(B - 1, 1, has_next=False, has_second=False)
            if elu:
                elu_exp(B - 1)

        @block.gpsimd
        def _(pool):
            def inverse_root(b):
                n = done + b
                wait_alone(pool, g.pool_passed, s["var_ready"], n + 1)
                nc.gpsimd.tensor_tensor(rstd[:], var_eps[:], g.minus_half[:], ALU.pow).then_inc(s["rstd"], 1)

            def reduce_max(b, par):
                n = done + b
                wait_alone(pool, g.pool_passed, s["cols_read"], n + 1)
                nc.gpsimd.partition_all_reduce(dmax[:, par:par + 1], dmax1[:], P,
                                               REDUCE_MAX).then_inc(s["dmax_ready"], 1)

            def make_addend(b, par):
                n = done + b
                wait_alone(pool, g.pool_passed, s["acc_read"], n - 1)
                dst = addend[:, par] if elu else spread[:]
                if not elu:
                    wait_alone(pool, g.pool_passed, s["addend_ready"], x_batches + b)
                last = nc.gpsimd.tensor_tensor(dst, empty[:].unsqueeze(2).to_broadcast([P, T, D]),
                                               mean_v[:, par:par + 1, :].to_broadcast([P, T, D]), ALU.mult)
                last.then_inc(s["empty_ready"], 1)
                if not elu:
                    wait_alone(pool, g.pool_passed, s["empty_ready"], n + 1)
                    last = nc.gpsimd.tensor_tensor(addend[:, par], spread[:], g.x[:, b], ALU.add)
                    last.then_inc(s["addend_ready"], 1)

            def elu_add(b):
                wait_alone(pool, g.pool_passed, s["elu_exp"], b + 1)
                nc.gpsimd.tensor_scalar(ex[:], ex[:], -1.0, None, ALU.add).then_inc(s["elu_less"], 1)
                wait_alone(pool, g.pool_passed, s["elu_less"], b + 1)
                nc.gpsimd.tensor_tensor(g.x[:, b], g.x[:, b], ex[:], ALU.add).then_inc(s["x_done"], 1)

            def step(b, par, has_next=True, has_second=True, has_before=True):
                if has_next:
                    reduce_max(b + 1, 1 - par)
                if has_second:
                    inverse_root(b + 2)
                if has_next:
                    make_addend(b + 1, 1 - par)
                if elu and has_before:
                    elu_add(b - 1)

            inverse_root(0)
            inverse_root(1)
            reduce_max(0, 0)
            make_addend(0, 0)
            step(0, 0, has_before=False)
            with pool.Fori(0, (B - 4) // 2) as j:
                step(2 * j + 1, 1)
                step(2 * j + 2, 0)
            step(B - 3, 1)
            step(B - 2, 0, has_second=False)
            step(B - 1, 1, has_next=False, has_second=False)
            if elu:
                elu_add(B - 1)

        @block.tensor
        def _(pe):
            def turn(b, par):
                n = done + b
                pe.wait_ge(s["normed"], n + 1)
                for it in range(T):
                    last = nc.tensor.transpose(aux[:, it // 4, (it % 4) * P:(it % 4 + 1) * P], hn[:, it, :],
                                               g.ident[:])
                last.then_inc(s["turned"], 1)

            def score_cols(b, par):
                n = done + b
                pe.wait_ge(s["h_ready"], n + 1)
                for jt in range(T):
                    nc.tensor.matmul(aux[:, 0, 2 * jt:2 * jt + 2], h_t[:, par, jt * P:(jt + 1) * P], wa,
                                     start=True, stop=True)
                nc.tensor.matmul(aux[:, 1, 0:D], h_sum[:, par:par + 1].to_broadcast([P, P]), w,
                                 start=True, stop=True).then_inc(s["cols_done"], 1)

            def source_row(b, par):
                n = done + b
                pe.wait_ge(s["cols_read"], n + 1)
                for half in range(2):
                    last = nc.tensor.matmul(aux[:, half, :], wa_rep, h_t[:, par, half * HALF:(half + 1) * HALF],
                                            start=True, stop=True)
                last.then_inc(s["src_done"], 1)

            def values(b, par):
                n = done + b
                pe.wait_ge(s["src_read"], n + 1)
                for jt in range(T):
                    last = nc.tensor.matmul(aux[:, jt // 4, (jt % 4) * D:(jt % 4 + 1) * D],
                                            h_t[:, par, jt * P:(jt + 1) * P], w, start=True, stop=True)
                last.then_inc(s["v_done"], 1)

            def products(b, par, k):
                n = done + b
                if k == 0:
                    pe.wait_ge(s["v_ready"], n + 1)
                    wait_for(pe, s["acc_read"], n - 1)
                pe.wait_ge(s["tile_ready"], T * n + k + 1)
                for it in range(T):
                    last = nc.tensor.matmul(acc(par, it, 0, V1), tiles[:, k % RING, it * P:(it + 1) * P],
                                            v[:, par, k, :], start=(k == 0 and it % 3 == 0), stop=(k == T - 1),
                                            skip_group_check=True)
                last.then_inc(s["tile_used"], 1)

            def step(b, par, has_next=True, has_second=True):
                for k in range(T):
                    products(b, par, k)
                    if k == 0 and has_next:
                        source_row(b + 1, 1 - par)
                    if k == 2 and has_next:
                        values(b + 1, 1 - par)
                    if k == 4 and has_second:
                        pe.wait_ge(s["v_ready"], done + b + 2)
                        turn(b + 2, par)
                    if k == 6 and has_second:
                        score_cols(b + 2, par)

            turn(0, 0)
            score_cols(0, 0)
            source_row(0, 0)
            values(0, 0)
            pe.wait_ge(s["v_ready"], done + 1)
            turn(1, 1)
            score_cols(1, 1)
            step(0, 0)
            with pe.Fori(0, (B - 4) // 2) as j:
                step(2 * j + 1, 1)
                step(2 * j + 2, 0)
            step(B - 3, 1)
            step(B - 2, 0, has_second=False)
            step(B - 1, 1, has_next=False, has_second=False)

        if layer == 3:
            @block.sync
            def _(sp):
                out_v = out_h.rearrange("b (t p) d -> p b t d", p=P)
                with sp.Fori(0, B) as b:
                    sp.wait_ge(s["acc_read"], done + b + 1)
                    sp.dma_start(out_v[:, b], g.x[:, b]).then_inc(out_done, 16)
                sp.wait_ge(out_done, 16 * B)


def head_layer(nc, g):
    with ExitStack() as ctx:
        def sb(name, shape, dt=FP32):
            return ctx.enter_context(nc.sbuf_tensor(name + "_l1", shape, dt))

        def sem(name):
            return ctx.enter_context(nc.semaphore("h_" + name))

        mask_off = sb("mask_off", [P, T, N], BF16)
        stats, mom = sb("stats", [P, T, 6]), sb("mom", [P, T, 2])
        var_eps, rstd = sb("var_eps", [P, T]), sb("rstd", [P, T])
        hn = sb("hn", [P, T, D])
        h_rest = sb("h_rest", [P, T, D])
        h_part = sb("h_part", [P, 3, T, D], BF16)
        h_t = sb("h_t", [P, N])
        off_t = sb("off_t", [P, N])
        row_rest = h_rest[0:2 * H].rearrange("p t d -> p (t d)")
        row_mid = hn[0:2 * H, 0:T // 2, :].rearrange("p t d -> p (t d)").bitcast(BF16)
        row_part = sb("row_part", [96, N], BF16)
        cols = sb("cols", [P, T, 2, H])
        dmax1, dmax, clamp = sb("dmax1", [P, H]), sb("dmax", [P, H]), sb("clamp", [P, H])
        top = sb("top", [P, T, H])
        args = sb("args", [P, 3, T, H])
        U, Q, R, MINUS_Q, C = range(5)
        batch_cols = sb("batch_cols", [P, 5, T, H])
        head_cols = sb("head_cols", [P, 2, 5, T])
        weights = sb("weights", [P, 2, T, H])
        weight_part = sb("weight_part", [P, T, H, 2, 3], BF16)
        head_part = sb("head_part", [P, 2, T, 2, 3], BF16)
        r_row = sb("r_row", [P, 2, N])
        v = sb("v", [P, 2, T, D])
        off = sb("off", [P, 2, T, D])
        tiles = sb("tiles", [P, RING, N])
        sign = sb("sign", [P, T, N], BF16)
        sums = sb("sums", [P, T + 1, 2])
        high, minus_den, recip, scale = sb("high", [P, T]), sb("minus_den", [P, T]), sb("recip", [P, T]), sb("scale", [P, T])
        ones = sb("ones", [P, P], BF16)
        z = sb("z", [P, 2, T, D])

        ps = ctx.enter_context(nc.psum_tensor("ps_l1", [P, 8, HALF], FP32))
        aux_a, aux_b = ps[:, 4:6, :], ps[:, 6, :]
        sums_ps = ps[:, 7, 0:(T + 1) * 6]

        stats_done, moments_done, var_ready, rstd_done, normed = (
            sem("stats"), sem("moments"), sem("var_ready"), sem("rstd"), sem("normed"))
        turned, h_ready, cols_done, cols_read, dmax_ready = (
            sem("turned"), sem("h_ready"), sem("cols_done"), sem("cols_read"), sem("dmax_ready"))
        top_ready, half_args, args_ready, exps_ready = sem("top"), sem("half_args"), sem("args"), sem("exps")
        weights_ready, high_part, weights_rest, mid_part, cols_ready = (
            sem("weights_ready"), sem("high_part"), sem("weights_rest"), sem("mid_part"), sem("cols_ready"))
        rows_done, hi_ready, rest_ready, mid_ready, mid_moved, rows_ready = (
            sem("rows_done"), sem("hi_ready"), sem("rest_ready"), sem("mid_ready"), sem("mid_moved"), sem("rows_ready"))
        relu_ready, rest1, part1, parts_ready = sem("relu_ready"), sem("rest1"), sem("part1"), sem("parts_ready")
        off_done, off_ready = sem("off_done"), sem("off_ready")
        off_mask_ready, ones_ready, part_zero = sem("off_mask_ready"), sem("ones_ready"), sem("part_zero")
        base_added = sem("base_added")
        head_ready, src_done, src_read, r_ready, v_done, v_ready = (
            sem("head_ready"), sem("src_done"), sem("src_read"), sem("r_ready"), sem("v_done"), sem("v_ready"))
        offv_done, offv_read = sem("offv_done"), sem("offv_read")
        sums_read, high_ready, den_ready = sem("sums_read"), sem("high_ready"), sem("den_ready")
        recip_ready, scale_ready, z_ready, tanh_ready, weighed, x_done = (
            sem("recip_ready"), sem("scale_ready"), sem("z_ready"), sem("tanh_ready"), sem("weighed"), sem("x_done"))
        tile_ready, tile_used, sign_ready, sign_used = (
            sem("tile_ready"), sem("tile_used"), sem("sign_ready"), sem("sign_used"))

        block = ctx.enter_context(nc.Block())

        def all_maps(eng, step):
            def pair(b, h, first=False, last=False, shared=False):
                step(b, h, 0, first=first, shared=shared)
                step(b, h + 1, 1, last=last, shared=shared)

            pair(0, 0, first=True)
            with eng.Fori(0, B - 1) as b:
                with eng.Fori(1, H // 2 - 1) as hp:
                    pair(b, 2 * hp)
                pair(b, H - 2, shared=True)
                pair(b + 1, 0)
            with eng.Fori(1, H // 2 - 1) as hp:
                pair(B - 1, 2 * hp)
            pair(B - 1, H - 2, last=True)

        def following(b, h):
            return (b + 1, 0) if isinstance(h, int) and h == H - 1 else (b, h + 1)

        @block.vector
        def _(dve):
            def norm(b):
                wait_for(dve, turned, b)
                wait_for(dve, relu_ready, b)
                wait_for(dve, mid_moved, b)
                for it in range(T):
                    last = nc.vector.bn_stats(stats[:, it, :], g.x[:, b, it, :])
                last.then_inc(stats_done, 1)
                wait_alone(dve, g.dve_passed, stats_done, b + 1)
                for it in range(T):
                    last = nc.vector.bn_aggr(mom[:, it, :], stats[:, it, :])
                last.then_inc(moments_done, 1)
                dve.wait_ge(moments_done, b + 1)
                nc.vector.tensor_scalar(var_eps[:], mom[:, :, 1], EPS, None, ALU.add).then_inc(var_ready, 1)
                dve.wait_ge(rstd_done, b + 1)
                for it in range(T):
                    last = nc.vector.tensor_scalar(hn[:, it, :], g.x[:, b, it, :], mom[:, it, 0:1],
                                                   rstd[:, it:it + 1], ALU.subtract, ALU.mult)
                last.then_inc(normed, 1)

            def read_cols(b):
                dve.wait_ge(cols_done, b + 1)
                nc.vector.tensor_reduce(dmax1[:], aux_b[:, 0:2 * T * H].rearrange(
                    "p (t c h) -> p c h t", t=T, c=2)[:, 1, :, :], AX_X, ALU.max)
                nc.vector.tensor_copy(cols[:].rearrange("p t c h -> p (t c h)"),
                                      aux_b[:, 0:2 * T * H]).then_inc(cols_read, 1)

            def exponents(b):
                dve.wait_ge(dmax_ready, b + 1)
                dve.wait_ge(cols_read, b + 1)
                over_tiles = dmax[:].unsqueeze(1).to_broadcast([P, T, H])
                nc.vector.tensor_tensor(top[:], cols[:, :, 0, :], over_tiles, ALU.add)
                nc.vector.tensor_scalar(clamp[:], dmax[:], -1.0, T_MAX, ALU.mult, ALU.add)
                nc.vector.tensor_tensor(args[:, 0], cols[:, :, 1, :], over_tiles, ALU.subtract).then_inc(top_ready, 1)
                dve.wait_ge(top_ready, b + 1)
                nc.vector.tensor_copy(batch_cols[:, C], clamp[:].unsqueeze(1).to_broadcast([P, T, H]))
                nc.vector.tensor_scalar(args[:, 1], args[:, 0], -RISE, Q_MAX, ALU.mult, ALU.min)
                nc.vector.tensor_scalar(args[:, 2], top[:], T_MAX, RISE, ALU.min, ALU.mult).then_inc(half_args, 1)
                dve.wait_ge(half_args, b + 1)
                nc.vector.tensor_scalar(args[:, 0], args[:, 0], SHIFT, None, ALU.add)
                nc.vector.tensor_scalar(args[:, 1:3], args[:, 1:3], -SHIFT, None, ALU.add).then_inc(args_ready, 1)

            def split_weights(b):
                dve.wait_ge(exps_ready, b + 1)
                nc.vector.tensor_scalar(batch_cols[:, MINUS_Q], batch_cols[:, Q], -1.0, None, ALU.mult)
                nc.vector.tensor_copy(weights[:, 0], batch_cols[:, U])
                nc.vector.tensor_tensor(weights[:, 1], batch_cols[:, U], batch_cols[:, Q],
                                        ALU.mult).then_inc(weights_ready, 1)
                dve.wait_ge(weights_ready, b + 1)
                part = weight_part[:].rearrange("p t h c w -> p c (t h) w")
                left = weights[:].rearrange("p c t h -> p c (t h)")
                nc.vector.tensor_copy(part[:, :, :, 0], left).then_inc(high_part, 1)
                dve.wait_ge(high_part, b + 1)
                nc.vector.tensor_tensor(left, left, part[:, :, :, 0], ALU.subtract).then_inc(weights_rest, 1)
                dve.wait_ge(weights_rest, b + 1)
                nc.vector.tensor_copy(part[:, :, :, 1], left).then_inc(mid_part, 1)
                dve.wait_ge(mid_part, b + 1)
                nc.vector.tensor_tensor(part[:, :, :, 2], left, part[:, :, :, 1], ALU.subtract).then_inc(cols_ready, 1)

            def split_rows(b):
                dve.wait_ge(rows_done, b + 1)
                dve.wait_ge(parts_ready, b + 1)
                dve.wait_ge(turned, b + 1)
                wait_for(dve, src_done, 2 * H * b)
                if isinstance(b, int) and b == 0:
                    dve.wait_ge(part_zero, 1)
                rows = aux_a[0:2 * H]
                hi = row_part[0:2 * H, :].rearrange("p (a n) -> p a n", a=2)
                nc.vector.tensor_copy(hi, rows).then_inc(hi_ready, 1)
                dve.wait_ge(hi_ready, b + 1)
                nc.vector.tensor_tensor(row_rest.rearrange("p (a n) -> p a n", a=2), rows, hi,
                                        ALU.subtract).then_inc(rest_ready, 1)
                dve.wait_ge(rest_ready, b + 1)
                nc.vector.tensor_copy(row_mid, row_rest).then_inc(mid_ready, 1)
                dve.wait_ge(mid_ready, b + 1)
                nc.vector.tensor_tensor(row_part[64:64 + 2 * H, :], row_rest, row_mid,
                                        ALU.subtract).then_inc(rows_ready, 1)

            def take_head(b, h, par):
                m = H * b + h
                dve.wait_ge(cols_ready, b + 1)
                wait_for(dve, sign_used, T * (m - 1))
                nc.vector.tensor_copy(head_part[:, par], weight_part[:, :, bass.ds(h, 1)]
                                      .rearrange("p t o c w -> p t (o c) w"))
                nc.vector.tensor_copy(head_cols[:, par], batch_cols[:, :, :, bass.ds(h, 1)]
                                      .rearrange("p c t o -> p c (t o)")).then_inc(head_ready, 1)

            def values(b, h, par):
                m = H * b + h
                dve.wait_ge(v_done, m + 1)
                dve.wait_ge(head_ready, m + 1)
                for half in range(2):
                    ts = slice(4 * half, 4 * half + 4)
                    last = nc.vector.tensor_tensor(
                        v[:, par, ts, :], aux_a[:, half, :].rearrange("p (t d) -> p t d", d=D),
                        head_cols[:, par, U, ts].unsqueeze(2).to_broadcast([P, 4, D]), ALU.mult)
                last.then_inc(v_ready, 1)

            def tile(m, par, k):
                if k == 0:
                    dve.wait_ge(r_ready, m + 1)
                wait_for(dve, tile_used, T * m + k - RING + 1)
                nc.vector.scalar_tensor_tensor(tiles[:, k % RING, :], r_row[:, par, :], head_cols[:, par, Q, k:k + 1],
                                               g.mask_gt[:, k, :], ALU.max, ALU.mult).then_inc(tile_ready, 1)

            def finish(m, par):
                dve.wait_ge(sign_used, T * (m + 1))
                nc.vector.tensor_reduce(sums[:].rearrange("p t c -> p (t c)"),
                                        sums_ps.rearrange("p (t w) -> p t w", w=3), AX_X, ALU.add).then_inc(sums_read, 1)
                dve.wait_ge(sums_read, m + 1)
                nc.vector.scalar_tensor_tensor(high[:], sums[:, 0:T, 0], sums[:, T, 0:1], head_cols[:, par, R, :],
                                               ALU.add, ALU.mult).then_inc(high_ready, 1)
                dve.wait_ge(high_ready, m + 1)
                nc.vector.scalar_tensor_tensor(minus_den[:], sums[:, 0:T, 1], sums[:, T, 1:2], high[:],
                                               ALU.subtract, ALU.subtract).then_inc(den_ready, 1)
                dve.wait_ge(den_ready, m + 1)
                nc.vector.reciprocal(recip[:], minus_den[:]).then_inc(recip_ready, 1)
                dve.wait_ge(recip_ready, m + 1)
                nc.vector.tensor_scalar(scale[:], recip[:], -2.0, None, ALU.mult).then_inc(scale_ready, 1)
                dve.wait_ge(scale_ready, m + 1)
                dve.wait_ge(tile_used, T * (m + 1))
                dve.wait_ge(offv_read, m + 1)
                wait_for(dve, x_done, m - 1)
                for it in range(T):
                    last = nc.vector.scalar_tensor_tensor(
                        z[:, par, it, :], ps[:, 2 * par + it // 4, (it % 4) * D:(it % 4 + 1) * D],
                        scale[:, it:it + 1], off[:, par, it, :], ALU.mult, ALU.add)
                last.then_inc(z_ready, 1)

            def step(b, h, par, first=False, last=False, shared=False):
                m = H * b + h
                b1, h1 = following(b, h)
                for k in range(T):
                    tile(m, par, k)
                    if k == 1 and shared and par == 0:
                        norm(b + 1)
                    if k == 3:
                        if not first:
                            finish(m - 1, 1 - par)
                        if shared and par == 1:
                            read_cols(b + 1)
                        elif not last:
                            take_head(b1, h1, 1 - par)
                    if k == 4 and shared and par == 1:
                        exponents(b + 1)
                        split_rows(b + 1)
                        split_weights(b + 1)
                        take_head(b1, h1, 1 - par)
                    if k == (7 if shared and par == 1 else 5) and not last:
                        values(b1, h1, 1 - par)

            nc.vector.tensor_scalar(mask_off[:], g.mask_gt[:], -1.0, 1.0, ALU.mult, ALU.add).then_inc(off_mask_ready, 1)
            norm(0)
            read_cols(0)
            exponents(0)
            split_rows(0)
            split_weights(0)
            take_head(0, 0, 0)
            values(0, 0, 0)
            all_maps(dve, step)
            finish(B * H - 1, 1)

        @block.scalar
        def _(act):
            def relu_h(b):
                act.wait_ge(turned, b + 1)
                wait_for(act, v_done, H * b)
                nc.scalar.activation(h_t[:].rearrange("p (a n) -> p a n", a=2), aux_a, ACT.Relu).then_inc(h_ready, 1)

            def exps(b):
                act.wait_ge(args_ready, b + 1)
                wait_for(act, head_ready, H * b)
                nc.scalar.activation(batch_cols[:, U:R + 1], args[:], ACT.Exp).then_inc(exps_ready, 1)

            def move_mid(b):
                act.wait_ge(mid_ready, b + 1)
                wait_for(act, src_done, 2 * H * b)
                if isinstance(b, int) and b == 0:
                    act.wait_ge(part_zero, 1)
                nc.scalar.activation(row_part[32:32 + 2 * H, :], row_mid, ACT.Copy).then_inc(mid_moved, 1)

            def off_rows(b, half):
                act.wait_ge(off_done, 2 * b + half + 1)
                wait_for(act, offv_done, H * b)
                nc.scalar.activation(off_t[:, half * HALF:(half + 1) * HALF], aux_b, ACT.Copy,
                                     scale=NEG_BIG).then_inc(off_ready, 1)

            def source(m, par, half):
                act.wait_ge(head_ready, m + 1)
                act.wait_ge(src_done, 2 * m + half + 1)
                wait_for(act, tile_ready, T * (m - 1))
                nc.scalar.activation(r_row[:, par, half * HALF:(half + 1) * HALF], aux_b, ACT.Relu,
                                     bias=head_cols[:, par, C, 0:1], scale=-1.0).then_inc(src_read, 1)

            def r_exp(m, par):
                act.wait_ge(src_read, 2 * m + 2)
                nc.scalar.activation(r_row[:, par, :], r_row[:, par, :], ACT.Exp, bias=g.bias_r[:],
                                     scale=-RISE).then_inc(r_ready, 1)

            def off_values(m, par):
                act.wait_ge(offv_done, m + 1)
                wait_for(act, z_ready, m - 1)
                nc.scalar.activation(off[:, par].rearrange("p (a t) d -> p a (t d)", a=2), aux_a,
                                     ACT.Copy).then_inc(offv_read, 1)

            def signs(m, par, k):
                if k == 0:
                    act.wait_ge(r_ready, m + 1)
                wait_for(act, sign_used, T * (m - 1) + k + 1)
                nc.scalar.activation(sign[:, k, :], r_row[:, par, :], ACT.Sign,
                                     bias=head_cols[:, par, MINUS_Q, k:k + 1]).then_inc(sign_ready, 1)

            def tanh(m, par):
                act.wait_ge(z_ready, m + 1)
                nc.scalar.activation(z[:, par], z[:, par], ACT.Tanh, scale=0.5).then_inc(tanh_ready, 1)

            def step(b, h, par, first=False, last=False, shared=False):
                m = H * b + h
                last_head = shared and par == 1
                for k in range(T):
                    signs(m, par, k)
                    if last_head:
                        if k == 1:
                            off_rows(b + 1, 0)
                        if k == 3:
                            off_rows(b + 1, 1)
                            exps(b + 1)
                            move_mid(b + 1)
                    if not last:
                        if k == (5 if last_head else 2):
                            source(m + 1, 1 - par, 0)
                        if k == (6 if last_head else 3):
                            source(m + 1, 1 - par, 1)
                            r_exp(m + 1, 1 - par)
                        if k == (7 if last_head else 5):
                            off_values(m + 1, 1 - par)
                    if k == (7 if last_head else 4) and not first:
                        tanh(m - 1, 1 - par)
                if shared and par == 0:
                    relu_h(b + 1)

            relu_h(0)
            exps(0)
            move_mid(0)
            off_rows(0, 0)
            off_rows(0, 1)
            source(0, 0, 0)
            source(0, 0, 1)
            r_exp(0, 0)
            off_values(0, 0)
            all_maps(act, step)
            tanh(B * H - 1, 1)

        @block.gpsimd
        def _(pool):
            def shared(b):
                wait_alone(pool, g.pool_passed, normed, b + 1)
                wait_alone(pool, g.pool_passed, off_done, 2 * b)
                wait_alone(pool, g.pool_passed, rows_ready, b)
                nc.gpsimd.tensor_scalar(h_part[:, 0], hn[:], 0.0, None, ALU.max)
                nc.gpsimd.tensor_scalar(h_rest[:], hn[:], 0.0, None, ALU.max).then_inc(relu_ready, 1)
                wait_alone(pool, g.pool_passed, relu_ready, b + 1)
                nc.gpsimd.tensor_tensor(h_rest[:], h_rest[:], h_part[:, 0], ALU.subtract).then_inc(rest1, 1)
                wait_alone(pool, g.pool_passed, rest1, b + 1)
                nc.gpsimd.tensor_copy(h_part[:, 1], h_rest[:]).then_inc(part1, 1)
                wait_alone(pool, g.pool_passed, part1, b + 1)
                nc.gpsimd.tensor_tensor(h_part[:, 2], h_rest[:], h_part[:, 1], ALU.subtract).then_inc(parts_ready, 1)
                nc.gpsimd.tensor_tensor(g.x[:, b], g.x[:, b], g.base1[:].unsqueeze(2).to_broadcast([P, T, D]), ALU.add).then_inc(base_added, 1)

            def inverse_root(b):
                wait_alone(pool, g.pool_passed, var_ready, b + 1)
                nc.gpsimd.tensor_tensor(rstd[:], var_eps[:], g.minus_half[:], ALU.pow).then_inc(rstd_done, 1)

            def reduce_max(b):
                wait_alone(pool, g.pool_passed, cols_read, b + 1)
                nc.gpsimd.partition_all_reduce(dmax[:], dmax1[:], P, REDUCE_MAX).then_inc(dmax_ready, 1)

            def weigh(b, h, m, par):
                wait_alone(pool, g.pool_passed, tanh_ready, m + 1)
                nc.gpsimd.tensor_tensor(z[:, par], z[:, par],
                                        g.half_w[:, bass.ds(h, 1)].unsqueeze(2).to_broadcast([P, T, D]), ALU.mult).then_inc(weighed, 1)
                wait_alone(pool, g.pool_passed, weighed, m + 1)
                wait_alone(pool, g.pool_passed, base_added, b + 1)
                wait_alone(pool, g.pool_passed, x_done, m)
                nc.gpsimd.tensor_tensor(g.x[:, b], g.x[:, b], z[:, par], ALU.add).then_inc(x_done, 1)

            def step(b, h, par, first=False, last=False, shared_=False, **kw):
                is_shared = kw.get("shared", False)
                m = H * b + h
                if is_shared and par == 0:
                    inverse_root(b + 1)
                    shared(b + 1)
                if not first:
                    if isinstance(h, int) and h == 0:
                        weigh(b - 1, H - 1, m - 1, 1 - par)
                    else:
                        weigh(b, h - 1, m - 1, 1 - par)
                if is_shared and par == 0:
                    reduce_max(b + 1)

            nc.gpsimd.memset(ones[:], 1.0).then_inc(ones_ready, 1)
            nc.gpsimd.memset(row_part[:], 0.0).then_inc(part_zero, 1)
            inverse_root(0)
            shared(0)
            reduce_max(0)
            all_maps(pool, step)
            weigh(B - 1, H - 1, B * H - 1, 1)

        @block.tensor
        def _(pe):
            def turn(b):
                pe.wait_ge(normed, b + 1)
                wait_for(pe, offv_read, H * b)
                for it in range(T):
                    last = nc.tensor.transpose(aux_a[:, it // 4, (it % 4) * P:(it % 4 + 1) * P], hn[:, it, :],
                                               g.ident[:])
                last.then_inc(turned, 1)

            def score_cols(b):
                pe.wait_ge(h_ready, b + 1)
                wait_for(pe, src_read, 2 * H * b)
                for jt in range(T):
                    last = nc.tensor.matmul(aux_b[:, 2 * H * jt:2 * H * (jt + 1)], h_t[:, jt * P:(jt + 1) * P],
                                            g.wa_heads[:].rearrange("p c h -> p (c h)"), start=True, stop=True)
                last.then_inc(cols_done, 1)

            def score_rows(b):
                pe.wait_ge(h_ready, b + 1)
                for half in range(2):
                    last = nc.tensor.matmul(aux_a[0:2 * H, half, :], g.wa_heads[:].rearrange("p c h -> p (c h)"),
                                            h_t[:, half * HALF:(half + 1) * HALF], start=True, stop=True)
                last.then_inc(rows_done, 1)

            def off_sums(b, half):
                if half == 0:
                    pe.wait_ge(parts_ready, b + 1)
                    pe.wait_ge(off_mask_ready, 1)
                    pe.wait_ge(cols_read, b + 1)
                else:
                    pe.wait_ge(off_ready, 2 * b + 1)
                for jt in range(T):
                    for part in range(3):
                        last = nc.tensor.matmul(aux_b, h_part[:, part, jt, :],
                                                mask_off[:, jt, half * HALF:(half + 1) * HALF],
                                                start=(jt == 0 and part == 0), stop=(jt == T - 1 and part == 2))
                last.then_inc(off_done, 1)

            def source(b, h, m, half, new_batch):
                if half == 1:
                    pe.wait_ge(src_read, 2 * m + 1)
                elif new_batch:
                    pe.wait_ge(off_ready, 2 * b + 2)
                    pe.wait_ge(rows_ready, b + 1)
                    pe.wait_ge(mid_moved, b + 1)
                else:
                    pe.wait_ge(src_read, 2 * m)
                nc.tensor.matmul(aux_b, g.sel[0:96, bass.ds(h, 1), :].rearrange("k o p -> k (o p)"),
                                 row_part[:, half * HALF:(half + 1) * HALF], start=True,
                                 stop=True).then_inc(src_done, 1)

            def values(b, h, m, new_batch):
                if new_batch:
                    pe.wait_ge(rest_ready, b + 1)
                else:
                    pe.wait_ge(offv_read, m)
                wh = g.w_in[:, bass.ds(h + W_HEADS, 1), :].rearrange("p o d -> p (o d)")
                for jt in range(T):
                    last = nc.tensor.matmul(aux_a[:, jt // 4, (jt % 4) * D:(jt % 4 + 1) * D],
                                            h_t[:, jt * P:(jt + 1) * P], wh, start=True, stop=True)
                last.then_inc(v_done, 1)

            def off_values(b, h, m):
                pe.wait_ge(v_ready, m + 1)
                wh = g.w_in[:, bass.ds(h + W_HEADS, 1), :].rearrange("p o d -> p (o d)")
                for it in range(T):
                    last = nc.tensor.matmul(aux_a[:, it // 4, (it % 4) * D:(it % 4 + 1) * D],
                                            off_t[:, it * P:(it + 1) * P], wh, start=True, stop=True)
                last.then_inc(offv_done, 1)

            def sign_sums(m, par, k):
                if k == 0:
                    pe.wait_ge(head_ready, m + 1)
                    wait_for(pe, sums_read, m)
                    if isinstance(m, int) and m == 0:
                        pe.wait_ge(ones_ready, 1)
                    for jt in range(T):
                        nc.tensor.matmul(sums_ps[:, 6 * T:6 * T + 6], ones[:],
                                         head_part[:, par, jt].rearrange("p c w -> p (c w)"),
                                         start=(jt == 0), stop=(jt == T - 1), skip_group_check=True)
                pe.wait_ge(sign_ready, T * m + k + 1)
                for it in range(T):
                    last = nc.tensor.matmul(sums_ps[:, 6 * it:6 * it + 6], sign[:, k, it * P:(it + 1) * P],
                                            head_part[:, par, k].rearrange("p c w -> p (c w)"),
                                            start=False, stop=(k == T - 1), skip_group_check=True)
                last.then_inc(sign_used, 1)

            def products(m, par, k):
                if k == 0:
                    pe.wait_ge(v_ready, m + 1)
                    wait_for(pe, z_ready, m - 1)
                pe.wait_ge(tile_ready, T * m + k + 1)
                for it in range(T):
                    last = nc.tensor.matmul(ps[:, 2 * par + it // 4, (it % 4) * D:(it % 4 + 1) * D],
                                            tiles[:, k % RING, it * P:(it + 1) * P], v[:, par, k, :],
                                            start=(k == 0 and it % 4 == 0), stop=(k == T - 1), skip_group_check=True)
                last.then_inc(tile_used, 1)

            def step(b, h, par, first=False, last=False, shared=False):
                m = H * b + h
                b1, h1 = following(b, h)
                last_head = shared and par == 1
                for k in range(T):
                    products(m, par, k)
                    if last_head:
                        if k == 0:
                            score_rows(b + 1)
                        if k == 1:
                            off_sums(b + 1, 0)
                        if k == 2:
                            off_sums(b + 1, 1)
                    if not last:
                        if k == (5 if last_head else 2):
                            source(b1, h1, m + 1, 0, last_head)
                            values(b1, h1, m + 1, last_head)
                        if k == (6 if last_head else 3):
                            source(b1, h1, m + 1, 1, last_head)
                        if k == (7 if last_head else 4):
                            off_values(b1, h1, m + 1)
                    if k >= 2:
                        for j in ((0,), (1,), (2, 3), (4,), (5, 6), (7,))[k - 2]:
                            sign_sums(m, par, j)
                    if shared and par == 0:
                        if k == 6:
                            turn(b + 1)
                        if k == 7:
                            score_cols(b + 1)

            turn(0)
            score_cols(0)
            score_rows(0)
            off_sums(0, 0)
            off_sums(0, 1)
            source(0, 0, 0, 0, True)
            source(0, 0, 0, 1, True)
            values(0, 0, 0, True)
            off_values(0, 0, 0)
            all_maps(pe, step)


def gat_stack(nc, x_h, adj_h, w_in_h, w_out_h, a_h, avg_w_h, avg_b_h, out_h):
    with ExitStack() as ctx:
        def sb(name, shape, dt=FP32):
            return ctx.enter_context(nc.sbuf_tensor(name, shape, dt))

        g = Shared()
        g.x = sb("x_all", [P, B, T, D])
        g.mask_gt = sb("mask_gt", [P, T, N], BF16)
        g.mask_ne = sb("mask_ne", [P, T, N], UINT8)
        g.w_in = sb("w_in", [P, W_HEADS + H, D])
        g.wa = sb("wa", [P, W_HEADS + H, 2])
        g.wa_heads = sb("wa_heads", [P, 2, H])
        g.ident = sb("ident", [P, P])
        g.sel = sb("sel", [P, H, P], BF16)
        g.empty_gt, g.empty_ne = sb("empty_gt", [P, T]), sb("empty_ne", [P, T])
        g.avg_w, g.avg_b = sb("avg_w", [P, H]), sb("avg_b", [P, 1])
        g.half_w, g.half_sum, g.base1 = sb("half_w", [P, H]), sb("half_sum", [P, 1]), sb("base1", [P, 1])
        g.minus_half = sb("minus_half", [P, T])
        g.bias_up, g.bias_down, g.bias_r = sb("bias_up", [P, 1]), sb("bias_down", [P, 1]), sb("bias_r", [P, 1])

        g.pool_passed = ctx.enter_context(nc.semaphore("pool_passed"))
        g.dve_passed = ctx.enter_context(nc.semaphore("dve_passed"))

        setup(nc, g, (x_h, adj_h, w_in_h, w_out_h, a_h, avg_w_h, avg_b_h))
        s = masked_semaphores(nc, ctx)
        masked_layer(nc, g, s, 0, 0, out_h)
        head_layer(nc, g)
        masked_layer(nc, g, s, 2, 1, out_h)
        masked_layer(nc, g, s, 3, 2, out_h)


def kernel(x, adj, L0_gnn_W, L0_gnn_a, L1_gnn_W, L1_gnn_a, L1_gnn_avg_w, L1_gnn_avg_b, L2_gnn_W, L2_gnn_a,
           L3_gnn_W, L3_gnn_a):
    import numpy as np
    import concourse.bacc as bacc
    from concourse.bass_utils import run_bass_kernel_spmd

    w0, w1, w2, w3 = (np.asarray(w) for w in (L0_gnn_W, L1_gnn_W, L2_gnn_W, L3_gnn_W))
    w_in = np.concatenate([w0[:, None], w2.T[:, None], w3.T[:, None], w1.transpose(1, 0, 2)], axis=1)
    w_out = np.concatenate([w0.T[:, None], w2[:, None], w3[:, None], w1.transpose(2, 0, 1)], axis=1)
    a = np.stack([np.asarray(v).reshape(2, 128).T for v in (L0_gnn_a, L2_gnn_a, L3_gnn_a)]
                 + [np.asarray(L1_gnn_a)[h].reshape(2, 128).T for h in range(8)], axis=1)
    arrays = {
        "x_in": np.asarray(x), "adj_in": np.asarray(adj), "w_in_in": w_in, "w_out_in": w_out, "a_in": a,
        "avg_w_in": np.broadcast_to(np.asarray(L1_gnn_avg_w).reshape(1, 8), (128, 8)),
        "avg_b_in": np.broadcast_to(np.asarray(L1_gnn_avg_b).reshape(1, 1), (128, 1)),
    }
    arrays = {k: np.ascontiguousarray(v) for k, v in arrays.items()}
    nc = bacc.Bacc("TRN2", target_bir_lowering=False, num_devices=1)
    aps = [nc.dram_tensor(k, v.shape, mybir.dt.from_np(v.dtype), kind="ExternalInput").ap() for k, v in arrays.items()]
    out = nc.dram_tensor("out", (16, 1024, 128), FP32, kind="ExternalOutput").ap()
    gat_stack(nc, *aps, out)
    r = run_bass_kernel_spmd(nc, [arrays], core_ids=[0])
    return r.results[0]["out"]
```

```python
from contextlib import ExitStack

import concourse.bass as bass
from concourse import mybir

FP32 = mybir.dt.float32
BF16 = mybir.dt.bfloat16
INT32 = mybir.dt.int32
UINT8 = mybir.dt.uint8
ALU = mybir.AluOpType
ACT = mybir.ActivationFunctionType
AX_X = mybir.AxisListType.X
REDUCE_MAX = bass.bass_isa.ReduceOp.max

B = 16
N = 1024
D = 128
P = 128
T = N // P
H = 8
HALF = 512
RING = 4
EPS = 1e-5
SLOPE = 0.2
NEG_BIG = -9.0e15

RISE = 1.0 - SLOPE
SHIFT = 20.0
T_MAX = 93.0
Q_MAX = 105.0

W_ROW = {0: 0, 2: 1, 3: 2}
W_HEADS = 3


def wait_for(eng, sem, value):
    if isinstance(value, int) and value <= 0:
        return
    eng.wait_ge(sem, value)


def wait_alone(eng, passed, sem, value):
    wait_for(eng, sem, value)
    if not isinstance(value, int):
        eng.sem_inc(passed, 1)


class Shared:
    pass


def setup(nc, g, ins):
    x_h, adj_h, w_in_h, w_out_h, a_h, avg_w_h, avg_b_h = ins
    with ExitStack() as ctx:
        def sb(name, shape, dt):
            return ctx.enter_context(nc.sbuf_tensor(name, shape, dt))

        def sem(name):
            return ctx.enter_context(nc.semaphore(name))

        adj_rows = sb("adj_rows", [P, T, N], INT32)
        mask_rows = sb("mask_rows", [P, 2, 2, N], BF16)
        w_out = sb("w_out", [P, W_HEADS + H, D], FP32)
        a_cols = sb("a_cols", [P, W_HEADS + H, 2], FP32)
        row_count = sb("row_count", [P, 2, T], FP32)
        counted = sb("counted", [P, 4, N], BF16)
        ident_bf = sb("ident_bf", [P, P], BF16)
        mask_ps = ctx.enter_context(nc.psum_tensor("mask_ps", [P, 4, N], BF16))
        wa_ps = ctx.enter_context(nc.psum_tensor("wa_ps", [P, HALF], FP32))

        adj_in = [sem(f"adj_in{i}") for i in range(T)]
        w_loaded = sem("w_loaded")
        ident_zero, ident_made, sel_zero, sel_made = sem("ident_zero"), sem("ident_made"), sem("sel_zero"), sem("sel_made")
        masks_made, masks_turned, mask1_copied, mask3_copied = (
            sem("masks_made"), sem("masks_turned"), sem("mask1_copied"), sem("mask3_copied"))
        wa_done, wa_copied, rows_counted, ident_bf_made = sem("wa_done"), sem("wa_copied"), sem("rows_counted"), sem("ident_bf_made")

        block = ctx.enter_context(nc.Block())

        @block.sync
        def _(sp):
            for it in range(T):
                sp.dma_start(adj_rows[:, it, :], adj_h[it * P:(it + 1) * P, :]).then_inc(adj_in[it], 16)
            for c in range(4):
                sp.dma_start(g.x[:, 4 * c:4 * c + 4, :, :], x_h[4 * c:4 * c + 4].rearrange("b (t p) d -> p b t d", p=P)
                             ).then_inc(g.x_first if c == 0 else g.x_rest, 16)

        @block.scalar
        def _(act):
            act.dma_start(w_out[:], w_out_h).then_inc(w_loaded, 16)
            act.dma_start(a_cols[:], a_h).then_inc(w_loaded, 16)
            act.dma_start(g.w_in[:], w_in_h).then_inc(w_loaded, 16)
            act.dma_start(g.avg_w[:], avg_w_h).then_inc(w_loaded, 16)
            act.dma_start(g.avg_b[:], avg_b_h).then_inc(w_loaded, 16)
            for it in range(T):
                act.wait_ge(masks_made, it + 1)
                for kind in range(2):
                    if it >= 2:
                        act.wait_ge(rows_counted, 2 * it + kind - 3)
                    nc.scalar.activation(counted[:, (2 * it + kind) % 4], mask_rows[:, it % 2, kind, :], ACT.Copy,
                                         accum_out=row_count[:, kind, it:it + 1]).then_inc(rows_counted, 1)
                act.wait_ge(masks_turned, 2 * it + 1)
                nc.scalar.activation(g.mask_gt[:, :, it * P:(it + 1) * P],
                                     mask_ps[:, (2 * it) % 4, :].rearrange("p (t i) -> p t i", t=T),
                                     ACT.Copy).then_inc(mask1_copied, 1)

        @block.gpsimd
        def _(pool):
            nc.gpsimd.memset(g.ident[:], 0.0).then_inc(ident_zero, 1)
            pool.wait_ge(ident_zero, 1)
            nc.gpsimd.affine_select(out=g.ident[:], in_=g.ident[:], compare_op=ALU.not_equal, fill=1.0, base=0,
                                    pattern=[[-1, P]], channel_multiplier=1).then_inc(ident_made, 1)
            nc.gpsimd.memset(g.sel[:], 0.0).then_inc(sel_zero, 1)
            pool.wait_ge(sel_zero, 1)
            for part in range(3):
                nc.gpsimd.affine_select(out=g.sel[:], in_=g.sel[:], compare_op=ALU.not_equal, fill=1.0,
                                        base=-32 * part, pattern=[[-1, H], [0, P]],
                                        channel_multiplier=1).then_inc(sel_made, 1)
                pool.wait_ge(sel_made, part + 1)
            nc.gpsimd.memset(g.minus_half[:], -0.5)
            nc.gpsimd.memset(g.bias_up[:], SHIFT)
            nc.gpsimd.memset(g.bias_down[:], -SHIFT)
            nc.gpsimd.memset(g.bias_r[:], RISE * T_MAX - SHIFT)

        def copy_mask3(dve, it):
            dve.wait_ge(masks_turned, 2 * it + 2)
            nc.vector.tensor_copy(g.mask_ne[:, :, it * P:(it + 1) * P],
                                  mask_ps[:, (2 * it + 1) % 4, :].rearrange("p (t i) -> p t i", t=T)
                                  ).then_inc(mask3_copied, 1)

        @block.vector
        def _(dve):
            dve.wait_ge(ident_made, 1)
            nc.vector.tensor_copy(ident_bf[:], g.ident[:]).then_inc(ident_bf_made, 1)
            for it in range(T):
                dve.wait_ge(adj_in[it], 16)
                if it >= 2:
                    dve.wait_ge(masks_turned, 2 * (it - 1))
                    dve.wait_ge(rows_counted, 2 * (it - 1))
                rows = adj_rows[:, it, :]
                nc.vector.tensor_scalar(mask_rows[:, it % 2, 0, :], rows, 0.0, None, ALU.is_gt)
                nc.vector.tensor_scalar(mask_rows[:, it % 2, 1, :], rows, 0.0, None,
                                        ALU.not_equal).then_inc(masks_made, 1)
                if it >= 1:
                    copy_mask3(dve, it - 1)
            copy_mask3(dve, T - 1)
            dve.wait_ge(rows_counted, 2 * T)
            nc.vector.tensor_scalar(g.empty_gt[:], row_count[:, 0, :], 0.0, None, ALU.is_le)
            nc.vector.tensor_scalar(g.empty_ne[:], row_count[:, 1, :], 0.0, None, ALU.is_le)
            dve.wait_ge(wa_done, 1)
            nc.vector.tensor_copy(g.wa[:], wa_ps[:, 0:2 * (W_HEADS + H)].rearrange("p (l t) -> p l t", t=2))
            nc.vector.tensor_copy(g.wa_heads[:], wa_ps[:, 2 * W_HEADS:2 * (W_HEADS + H)]
                                  .rearrange("p (h t) -> p t h", t=2)).then_inc(wa_copied, 1)
            dve.wait_ge(wa_copied, 1)
            dve.wait_ge(w_loaded, 80)
            nc.vector.tensor_scalar(g.half_w[:], g.avg_w[:], 0.5, None, ALU.mult).then_inc(wa_copied, 1)
            dve.wait_ge(wa_copied, 2)
            nc.vector.tensor_reduce(g.half_sum[:], g.half_w[:], AX_X, ALU.add).then_inc(wa_copied, 1)
            dve.wait_ge(wa_copied, 3)
            nc.vector.tensor_tensor(g.base1[:], g.half_sum[:], g.avg_b[:], ALU.add)

        @block.tensor
        def _(pe):
            pe.wait_ge(ident_bf_made, 1)
            for it in range(T):
                pe.wait_ge(masks_made, it + 1)
                for kind in range(2):
                    if it >= 2:
                        pe.wait_ge((mask1_copied, mask3_copied)[kind], it - 1)
                    for jt in range(T):
                        last = nc.tensor.transpose(mask_ps[:, (2 * it + kind) % 4, jt * P:(jt + 1) * P],
                                                   mask_rows[:, it % 2, kind, jt * P:(jt + 1) * P], ident_bf[:])
                    last.then_inc(masks_turned, 1)
            pe.wait_ge(w_loaded, 80)
            for row in range(W_HEADS + H):
                last = nc.tensor.matmul(wa_ps[:, 2 * row:2 * row + 2], w_out[:, row, :], a_cols[:, row, :],
                                        start=True, stop=True)
            last.then_inc(wa_done, 1)


def masked_semaphores(nc, ctx):
    names = ["stats", "moments", "var_ready", "rstd", "shift_ready", "h_ready", "turned", "ht_ready", "cols_done",
             "cols_read", "dmax_ready", "drop_ready", "args_ready", "u_ready", "q_ready", "r_col_ready", "row_done",
             "r_ready", "v_done", "v_ready", "tile_ready", "tile_used", "empty_ready", "addend_ready", "den_ready",
             "recip_ready", "acc_read", "low_ready", "elu_exp", "elu_less", "x_done"]
    return {n: ctx.enter_context(nc.semaphore("m_" + n)) for n in names}


class MaskedLayer:

    def __init__(self, g, layer, order):
        self.mask = g.mask_ne if layer == 3 else g.mask_gt
        self.empty = g.empty_ne if layer == 3 else g.empty_gt
        self.elu = layer == 2
        self.after_elu = layer == 3
        self.loads_x = layer == 0
        self.w = g.w_in[:, W_ROW[layer], :]
        self.wa = g.wa[:, W_ROW[layer], :]
        self.done = B * order
        self.normed = B * order + (1 if layer >= 2 else 0)
        self.addends = {0: 0, 2: B, 3: B}[layer]
        self.before = self.after = None
        self.early = None


class HeadLayer:
    after_elu = loads_x = False
    done = normed = B


def layer_moments(nc, g, s, dve, la, b):
    n = la.normed + b
    if isinstance(b, int) and la.loads_x and b < 4:
        dve.wait_ge(g.x_first, 16)
        if b == 3:
            dve.wait_ge(g.x_rest, 3 * 16)
    if la.after_elu:
        wait_for(dve, s["x_done"], b + 1)
    wait_for(dve, s["shift_ready"], n)
    for it in range(T):
        last = nc.vector.bn_stats(g.stats[:, it, :], g.x[:, b, it, :])
    last.then_inc(s["stats"], 1)
    wait_alone(dve, g.dve_passed, s["stats"], n + 1)
    for it in range(T):
        last = nc.vector.bn_aggr(g.mom[:, it, :], g.stats[:, it, :])
    last.then_inc(s["moments"], 1)
    dve.wait_ge(s["moments"], n + 1)
    nc.vector.tensor_scalar(g.minus_mean[:], g.mom[:, :, 0], -1.0, None, ALU.mult)
    nc.vector.tensor_scalar(g.var_eps[:], g.mom[:, :, 1], EPS, None, ALU.add).then_inc(s["var_ready"], 1)


def layer_inverse_root(nc, g, s, pool, la, b):
    n = la.normed + b
    wait_alone(pool, g.pool_passed, s["var_ready"], n + 1)
    wait_alone(pool, g.pool_passed, s["h_ready"], n)
    nc.gpsimd.tensor_tensor(g.rstd[:], g.var_eps[:], g.minus_half[:], ALU.pow).then_inc(s["rstd"], 1)
    wait_alone(pool, g.pool_passed, s["rstd"], n + 1)
    nc.gpsimd.tensor_tensor(g.shift[:], g.minus_mean[:], g.rstd[:], ALU.mult).then_inc(s["shift_ready"], 1)


def layer_norm(nc, g, s, act, la, b):
    act.wait_ge(s["shift_ready"], la.normed + b + 1)
    wait_for(act, s["turned"], la.done + b)
    for it in range(T):
        last = nc.scalar.activation(g.h[:, it, :], g.x[:, b, it, :], ACT.Relu, bias=g.shift[:, it:it + 1],
                                    scale=g.rstd[:, it:it + 1])
    last.then_inc(s["h_ready"], 1)


def masked_layers(nc, g, s, layers, early_norm, early, out_h):
    V1 = D + 1
    for one, two in zip(layers, layers[1:]):
        one.after, two.before = two, one
    layers[-1].early = early
    any_elu = any(la.elu for la in layers)

    with ExitStack() as ctx:
        def sb(name, shape, dt=FP32):
            return ctx.enter_context(nc.sbuf_tensor(f"{name}_m{layers[0].done}", shape, dt))

        h = g.h
        h_t = sb("h_t", [P, 2, N])
        h_sum = sb("h_sum", [P, 2])
        cols = sb("cols", [P, 2, T, 2])
        mean_v = sb("mean_v", [P, 2, D])
        dmax1, dmax = sb("dmax1", [P, 1]), sb("dmax", [P, 2])
        drop, rise, top = sb("drop", [P, 2, T]), sb("rise", [P, 2, T]), sb("top", [P, 2, T])
        q, r_col = sb("q", [P, 2, T]), sb("r_col", [P, 2, T])
        r_row = sb("r_row", [P, 2, N])
        v = sb("v", [P, 2, T, V1])
        tiles = sb("tiles", [P, RING, N])
        spread = sb("spread", [P, T, D])
        addend = sb("addend", [P, 2, T, D])
        den, recip = sb("den", [P, T]), sb("recip", [P, T])
        if any_elu:
            y, low, ex = sb("y", [P, T, D]), sb("low", [P, T, D]), sb("ex", [P, T, D])
        ps = ctx.enter_context(nc.psum_tensor(f"ps_m{layers[0].done}", [P, 8, HALF], FP32))
        aux = ps[:, 6:8, :]
        out_done = ctx.enter_context(nc.semaphore(f"out_done{layers[0].done}"))

        def acc(par, it, lo, hi):
            at = (it % 3) * V1
            return ps[:, 3 * par + it // 3, at + lo:at + hi]

        def halves(ap):
            return ap.rearrange("p (a n) -> p a n", a=2)

        def moved(la, b, by):
            if isinstance(b, int) and not 0 <= b + by < B:
                other = la.after if by > 0 else la.before
                return other and (other, (b + by) % B)
            return la, b + by

        def steps(eng, step):
            for la in layers:
                step(la, 0, 0)
                step(la, 1, 1)
                with eng.Fori(0, (B - 4) // 2) as j:
                    step(la, 2 * j + 2, 0)
                    step(la, 2 * j + 3, 1)
                step(la, B - 2, 0)
                step(la, B - 1, 1)

        def begin(f, by):
            def call(la, b, par):
                at = moved(la, b, by)
                if at:
                    f(*at, (par + by) % 2)
            return call

        def norming(f, eng):
            def call(la, b, par):
                at = moved(la, b, 2)
                if not at and la.early and b == B - 2:
                    at = (la.early, 0)
                if at:
                    f(nc, g, s, eng, *at)
            return call

        block = ctx.enter_context(nc.Block())
        first = layers[0]

        @block.vector
        def _(dve):
            def read_cols(la, b, par):
                n = la.done + b
                dve.wait_ge(s["cols_done"], n + 1)
                wait_for(dve, s["empty_ready"], n - 1)
                ps_cols = aux[:, 0, 0:2 * T].rearrange("p (t c) -> p t c", c=2)
                nc.vector.tensor_reduce(dmax1[:], aux[:, 0, 0:2 * T].rearrange("p (t c) -> p c t", c=2)[:, 1, :],
                                        AX_X, ALU.max)
                nc.vector.tensor_copy(cols[:, par], ps_cols)
                nc.vector.tensor_scalar(mean_v[:, par, :], aux[:, 1, 0:D], 1.0 / N, None,
                                        ALU.mult).then_inc(s["cols_read"], 1)

            def exponents(la, b, par):
                n = la.done + b
                dve.wait_ge(s["dmax_ready"], n + 1)
                wait_for(dve, s["r_col_ready"], n - 1)
                nc.vector.tensor_scalar(drop[:, par, :], cols[:, par, :, 1], dmax[:, par:par + 1], None,
                                        ALU.subtract).then_inc(s["drop_ready"], 1)
                nc.vector.tensor_scalar(top[:, par, :], cols[:, par, :, 0], dmax[:, par:par + 1], T_MAX, ALU.add,
                                        ALU.min)
                dve.wait_ge(s["drop_ready"], n + 1)
                nc.vector.tensor_scalar(rise[:, par, :], drop[:, par, :], -RISE, Q_MAX, ALU.mult,
                                        ALU.min).then_inc(s["args_ready"], 1)

            def tile(la, b, par, k):
                n = la.done + b
                if k == 0:
                    dve.wait_ge(s["q_ready"], n + 1)
                    dve.wait_ge(s["r_ready"], n + 1)
                wait_for(dve, s["tile_used"], T * n + k - RING + 1)
                nc.vector.scalar_tensor_tensor(tiles[:, k % RING, :], r_row[:, par, :], q[:, par, k:k + 1],
                                               la.mask[:, k, :], ALU.max, ALU.mult).then_inc(s["tile_ready"], 1)

            def finish(la, b, par):
                n = la.done + b
                dve.wait_ge(s["tile_used"], T * (n + 1))
                for bank in range(3):
                    lo, hi = 3 * bank, min(3 * bank + 3, T)
                    sums = ps[:, 3 * par + bank, 0:(hi - lo) * V1].rearrange("p (t c) -> p t c", c=V1)[:, :, D]
                    last = nc.vector.tensor_tensor(den[:, lo:hi], sums, la.empty[:, lo:hi], ALU.add)
                last.then_inc(s["den_ready"], 1)
                dve.wait_ge(s["den_ready"], n + 1)
                nc.vector.reciprocal(recip[:], den[:]).then_inc(s["recip_ready"], 1)
                dve.wait_ge(s["recip_ready"], n + 1)
                if la.elu:
                    dve.wait_ge(s["empty_ready"], n + 1)
                else:
                    dve.wait_ge(s["addend_ready"], la.addends + b + 1)
                for it in range(T):
                    dst = y[:, it, :] if la.elu else g.x[:, b, it, :]
                    last = nc.vector.scalar_tensor_tensor(dst, acc(par, it, 0, D), recip[:, it:it + 1],
                                                          addend[:, par, it, :], ALU.mult, ALU.add)
                last.then_inc(s["acc_read"], 1)
                if la.elu:
                    dve.wait_ge(s["acc_read"], n + 1)
                    wait_for(dve, s["elu_exp"], b)
                    nc.vector.tensor_scalar(low[:], y[:], 0.0, None, ALU.min)
                    nc.vector.scalar_tensor_tensor(g.x[:, b], y[:], 0.0, g.x[:, b], ALU.max,
                                                   ALU.add).then_inc(s["low_ready"], 1)

            def step(la, b, par):
                for k in range(T):
                    tile(la, b, par, k)
                    if k == 1:
                        norming(layer_moments, dve)(la, b, par)
                    if k == 2:
                        begin(read_cols, 1)(la, b, par)
                    if k == 3:
                        begin(exponents, 1)(la, b, par)
                    if k == 4:
                        begin(finish, -1)(la, b, par)

            if not early_norm:
                layer_moments(nc, g, s, dve, first, 0)
            layer_moments(nc, g, s, dve, first, 1)
            read_cols(first, 0, 0)
            exponents(first, 0, 0)
            steps(dve, step)
            finish(layers[-1], B - 1, 1)

        @block.scalar
        def _(act):
            def copy_ht(la, b, par):
                n = la.done + b
                act.wait_ge(s["turned"], n + 1)
                wait_for(act, s["v_done"], n - 1)
                nc.scalar.activation(halves(h_t[:, par, :]), aux, ACT.Copy,
                                     accum_out=h_sum[:, par:par + 1]).then_inc(s["ht_ready"], 1)

            def exps(la, b, par):
                n = la.done + b
                act.wait_ge(s["args_ready"], n + 1)
                wait_for(act, s["tile_used"], T * (n - 1))
                nc.scalar.activation(r_col[:, par, :], top[:, par, :], ACT.Exp, bias=g.bias_down[:],
                                     scale=RISE).then_inc(s["r_col_ready"], 1)
                nc.scalar.activation(q[:, par, :], rise[:, par, :], ACT.Exp,
                                     bias=g.bias_down[:]).then_inc(s["q_ready"], 1)
                nc.scalar.activation(v[:, par, :, D], drop[:, par, :], ACT.Exp,
                                     bias=g.bias_up[:]).then_inc(s["u_ready"], 1)

            def copy_row(la, b, par):
                n = la.done + b
                act.wait_ge(s["row_done"], n + 1)
                nc.scalar.activation(halves(r_row[:, par, :]), aux, ACT.Copy).then_inc(s["r_ready"], 1)

            def values(la, b, par):
                n = la.done + b
                act.wait_ge(s["v_done"], n + 1)
                act.wait_ge(s["u_ready"], n + 1)
                for jt in range(T):
                    last = nc.scalar.activation(v[:, par, jt, 0:D], aux[:, jt // 4, (jt % 4) * D:(jt % 4 + 1) * D],
                                                ACT.Copy, scale=v[:, par, jt, D:V1])
                last.then_inc(s["v_ready"], 1)

            def elu_exp(la, b, par):
                if not la.elu:
                    return
                act.wait_ge(s["low_ready"], b + 1)
                wait_for(act, s["x_done"], b)
                nc.scalar.activation(ex[:], low[:], ACT.Exp).then_inc(s["elu_exp"], 1)

            def step(la, b, par):
                begin(exps, 1)(la, b, par)
                begin(copy_row, 1)(la, b, par)
                begin(values, 1)(la, b, par)
                norming(layer_norm, act)(la, b, par)
                begin(elu_exp, -1)(la, b, par)
                begin(copy_ht, 2)(la, b, par)

            if not early_norm:
                layer_norm(nc, g, s, act, first, 0)
            copy_ht(first, 0, 0)
            layer_norm(nc, g, s, act, first, 1)
            exps(first, 0, 0)
            copy_row(first, 0, 0)
            values(first, 0, 0)
            copy_ht(first, 1, 1)
            steps(act, step)
            elu_exp(layers[-1], B - 1, 1)

        @block.gpsimd
        def _(pool):
            def reduce_max(la, b, par):
                n = la.done + b
                wait_alone(pool, g.pool_passed, s["cols_read"], n + 1)
                nc.gpsimd.partition_all_reduce(dmax[:, par:par + 1], dmax1[:], P,
                                               REDUCE_MAX).then_inc(s["dmax_ready"], 1)

            def make_addend(la, b, par):
                n = la.done + b
                wait_alone(pool, g.pool_passed, s["acc_read"], n - 1)
                dst = addend[:, par] if la.elu else spread[:]
                if not la.elu:
                    wait_alone(pool, g.pool_passed, s["addend_ready"], la.addends + b)
                last = nc.gpsimd.tensor_tensor(dst, la.empty[:].unsqueeze(2).to_broadcast([P, T, D]),
                                               mean_v[:, par:par + 1, :].to_broadcast([P, T, D]), ALU.mult)
                last.then_inc(s["empty_ready"], 1)
                if not la.elu:
                    if la.after_elu:
                        wait_alone(pool, g.pool_passed, s["x_done"], b + 1)
                    wait_alone(pool, g.pool_passed, s["empty_ready"], n + 1)
                    nc.gpsimd.tensor_tensor(addend[:, par], spread[:], g.x[:, b],
                                            ALU.add).then_inc(s["addend_ready"], 1)

            def elu_add(la, b, par):
                if not la.elu:
                    return
                wait_alone(pool, g.pool_passed, s["elu_exp"], b + 1)
                nc.gpsimd.tensor_scalar(ex[:], ex[:], -1.0, None, ALU.add).then_inc(s["elu_less"], 1)
                wait_alone(pool, g.pool_passed, s["elu_less"], b + 1)
                nc.gpsimd.tensor_tensor(g.x[:, b], g.x[:, b], ex[:], ALU.add).then_inc(s["x_done"], 1)

            def step(la, b, par):
                norming(layer_inverse_root, pool)(la, b, par)
                begin(reduce_max, 1)(la, b, par)
                begin(make_addend, 1)(la, b, par)
                begin(elu_add, -1)(la, b, par)

            if not early_norm:
                layer_inverse_root(nc, g, s, pool, first, 0)
            layer_inverse_root(nc, g, s, pool, first, 1)
            reduce_max(first, 0, 0)
            make_addend(first, 0, 0)
            steps(pool, step)
            elu_add(layers[-1], B - 1, 1)

        @block.tensor
        def _(pe):
            def turn(la, b, par):
                n = la.done + b
                pe.wait_ge(s["h_ready"], la.normed + b + 1)
                if isinstance(b, int) and b == 0 and la is first:
                    pass
                else:
                    pe.wait_ge(s["v_ready"], n)
                for it in range(T):
                    last = nc.tensor.transpose(aux[:, it // 4, (it % 4) * P:(it % 4 + 1) * P], h[:, it, :],
                                               g.ident[:])
                last.then_inc(s["turned"], 1)

            def score_cols(la, b, par):
                n = la.done + b
                pe.wait_ge(s["ht_ready"], n + 1)
                for jt in range(T):
                    nc.tensor.matmul(aux[:, 0, 2 * jt:2 * jt + 2], h_t[:, par, jt * P:(jt + 1) * P], la.wa,
                                     start=True, stop=True)
                nc.tensor.matmul(aux[:, 1, 0:D], h_sum[:, par:par + 1].to_broadcast([P, P]), la.w,
                                 start=True, stop=True).then_inc(s["cols_done"], 1)

            def source_row(la, b, par):
                n = la.done + b
                pe.wait_ge(s["cols_read"], n + 1)
                pe.wait_ge(s["r_col_ready"], n + 1)
                for it in range(T):
                    last = nc.tensor.transpose(aux[:, it // 4, (it % 4) * P:(it % 4 + 1) * P],
                                               r_col[:, par, it:it + 1].to_broadcast([P, P]), g.ident[:])
                last.then_inc(s["row_done"], 1)

            def values(la, b, par):
                n = la.done + b
                pe.wait_ge(s["r_ready"], n + 1)
                for jt in range(T):
                    last = nc.tensor.matmul(aux[:, jt // 4, (jt % 4) * D:(jt % 4 + 1) * D],
                                            h_t[:, par, jt * P:(jt + 1) * P], la.w, start=True, stop=True)
                last.then_inc(s["v_done"], 1)

            def products(la, b, par, k):
                n = la.done + b
                if k == 0:
                    pe.wait_ge(s["v_ready"], n + 1)
                    wait_for(pe, s["acc_read"], n - 1)
                pe.wait_ge(s["tile_ready"], T * n + k + 1)
                for it in range(T):
                    last = nc.tensor.matmul(acc(par, it, 0, V1), tiles[:, k % RING, it * P:(it + 1) * P],
                                            v[:, par, k, :], start=(k == 0 and it % 3 == 0), stop=(k == T - 1),
                                            skip_group_check=True)
                last.then_inc(s["tile_used"], 1)

            def step(la, b, par):
                for k in range(T):
                    products(la, b, par, k)
                    if k == 2:
                        begin(source_row, 1)(la, b, par)
                    if k == 3:
                        begin(values, 1)(la, b, par)
                    if k == 6:
                        begin(turn, 2)(la, b, par)
                    if k == 7:
                        begin(score_cols, 2)(la, b, par)

            turn(first, 0, 0)
            score_cols(first, 0, 0)
            source_row(first, 0, 0)
            values(first, 0, 0)
            turn(first, 1, 1)
            score_cols(first, 1, 1)
            steps(pe, step)

        if out_h is not None:
            last_layer = layers[-1]

            @block.sync
            def _(sp):
                out_v = out_h.rearrange("b (t p) d -> p b t d", p=P)
                with sp.Fori(0, B) as b:
                    sp.wait_ge(s["acc_read"], last_layer.done + b + 1)
                    sp.dma_start(out_v[:, b], g.x[:, b]).then_inc(out_done, 16)
                sp.wait_ge(out_done, 16 * B)


def head_layer(nc, g, s, next_layer):
    with ExitStack() as ctx:
        def sb(name, shape, dt=FP32):
            return ctx.enter_context(nc.sbuf_tensor(name + "_l1", shape, dt))

        def sem(name):
            return ctx.enter_context(nc.semaphore("h_" + name))

        mask_off = sb("mask_off", [P, T, N], BF16)
        stats, mom, var_eps, rstd = g.stats, g.mom, g.var_eps, g.rstd
        hn = g.h
        h_rest = sb("h_rest", [P, T, D])
        h_part = sb("h_part", [P, 3, T, D], BF16)
        h_t = sb("h_t", [P, N])
        off_t = sb("off_t", [P, N])
        row_rest = h_rest[0:2 * H].rearrange("p t d -> p (t d)")
        row_mid = hn[0:2 * H, 0:T // 2, :].rearrange("p t d -> p (t d)").bitcast(BF16)
        row_part = sb("row_part", [96, N], BF16)
        cols = sb("cols", [P, T, 2, H])
        dmax1, dmax, clamp = sb("dmax1", [P, H]), sb("dmax", [P, H]), sb("clamp", [P, H])
        top = sb("top", [P, T, H])
        args = sb("args", [P, 3, T, H])
        U, Q, R, MINUS_Q, C = range(5)
        batch_cols = sb("batch_cols", [P, 5, T, H])
        head_cols = sb("head_cols", [P, 2, 5, T])
        weights = sb("weights", [P, 2, T, H])
        weight_part = sb("weight_part", [P, T, H, 2, 3], BF16)
        head_part = sb("head_part", [P, 2, T, 2, 3], BF16)
        r_row = sb("r_row", [P, 2, N])
        v = sb("v", [P, 2, T, D])
        off = sb("off", [P, 2, T, D])
        tiles = sb("tiles", [P, RING, N])
        sign = sb("sign", [P, T, N], BF16)
        sums, totals, total = sb("sums", [P, T, 2]), sb("totals", [P, H, 2]), sb("total", [P, 2])
        high, minus_den, recip, scale = sb("high", [P, T]), sb("minus_den", [P, T]), sb("recip", [P, T]), sb("scale", [P, T])
        ones = sb("ones", [P, P], BF16)
        z = sb("z", [P, 2, T, D])

        ps = ctx.enter_context(nc.psum_tensor("ps_l1", [P, 8, HALF], FP32))
        aux_a, aux_b = ps[:, 4:6, :], ps[:, 6, :]
        sums_ps = ps[:, 7, 0:T * 6]
        totals_ps = ps[:, 7, T * 6:(T + H) * 6]

        stats_done, moments_done, var_ready, rstd_done, normed = (
            sem("stats"), sem("moments"), sem("var_ready"), sem("rstd"), sem("normed"))
        turned, h_ready, cols_done, cols_read, dmax_ready = (
            sem("turned"), sem("h_ready"), sem("cols_done"), sem("cols_read"), sem("dmax_ready"))
        top_ready, half_args, args_ready, exps_ready = sem("top"), sem("half_args"), sem("args"), sem("exps")
        weights_ready, high_part, weights_rest, mid_part, cols_ready = (
            sem("weights_ready"), sem("high_part"), sem("weights_rest"), sem("mid_part"), sem("cols_ready"))
        rows_done, hi_ready, rest_ready, mid_ready, mid_moved, rows_ready = (
            sem("rows_done"), sem("hi_ready"), sem("rest_ready"), sem("mid_ready"), sem("mid_moved"), sem("rows_ready"))
        relu_ready, rest1, part1, parts_ready = sem("relu_ready"), sem("rest1"), sem("part1"), sem("parts_ready")
        off_done, off_ready = sem("off_done"), sem("off_ready")
        off_mask_ready, ones_ready, part_zero = sem("off_mask_ready"), sem("ones_ready"), sem("part_zero")
        base_added = sem("base_added")
        head_ready, src_done, src_read, r_ready, v_done, v_ready = (
            sem("head_ready"), sem("src_done"), sem("src_read"), sem("r_ready"), sem("v_done"), sem("v_ready"))
        offv_done, offv_read = sem("offv_done"), sem("offv_read")
        totals_read = sem("totals_read")
        sums_read, high_ready, den_ready = sem("sums_read"), sem("high_ready"), sem("den_ready")
        recip_ready, scale_ready, z_ready, tanh_ready, weighed, x_done = (
            sem("recip_ready"), sem("scale_ready"), sem("z_ready"), sem("tanh_ready"), sem("weighed"), sem("x_done"))
        tile_ready, tile_used, sign_ready, sign_used = (
            sem("tile_ready"), sem("tile_used"), sem("sign_ready"), sem("sign_used"))

        block = ctx.enter_context(nc.Block())

        def all_maps(eng, step):
            def pair(b, h, first=False, last=False, shared=False):
                step(b, h, 0, first=first, shared=shared)
                step(b, h + 1, 1, last=last, shared=shared)

            pair(0, 0, first=True)
            with eng.Fori(0, B - 1) as b:
                with eng.Fori(1, H // 2 - 1) as hp:
                    pair(b, 2 * hp)
                pair(b, H - 2, shared=True)
                pair(b + 1, 0)
            with eng.Fori(1, H // 2 - 1) as hp:
                pair(B - 1, 2 * hp)
            pair(B - 1, H - 2, last=True)

        def following(b, h):
            return (b + 1, 0) if isinstance(h, int) and h == H - 1 else (b, h + 1)

        def before(b, h):
            return (b - 1, H - 1) if isinstance(h, int) and h == 0 else (b, h - 1)

        @block.vector
        def _(dve):
            def moments(b):
                for it in range(T):
                    last = nc.vector.bn_stats(stats[:, it, :], g.x[:, b, it, :])
                last.then_inc(stats_done, 1)
                wait_alone(dve, g.dve_passed, stats_done, b)
                for it in range(T):
                    last = nc.vector.bn_aggr(mom[:, it, :], stats[:, it, :])
                last.then_inc(moments_done, 1)
                dve.wait_ge(moments_done, b)
                nc.vector.tensor_scalar(var_eps[:], mom[:, :, 1], EPS, None, ALU.add).then_inc(var_ready, 1)

            def norm(b):
                wait_for(dve, turned, b)
                wait_for(dve, relu_ready, b)
                wait_for(dve, mid_moved, b)
                dve.wait_ge(rstd_done, b)
                for it in range(T):
                    last = nc.vector.tensor_scalar(hn[:, it, :], g.x[:, b, it, :], mom[:, it, 0:1],
                                                   rstd[:, it:it + 1], ALU.subtract, ALU.mult)
                last.then_inc(normed, 1)

            def read_cols(b):
                dve.wait_ge(cols_done, b + 1)
                nc.vector.tensor_reduce(dmax1[:], aux_b[:, 0:2 * T * H].rearrange(
                    "p (t c h) -> p c h t", t=T, c=2)[:, 1, :, :], AX_X, ALU.max)
                nc.vector.tensor_copy(cols[:].rearrange("p t c h -> p (t c h)"),
                                      aux_b[:, 0:2 * T * H]).then_inc(cols_read, 1)

            def exponents(b):
                dve.wait_ge(dmax_ready, b + 1)
                dve.wait_ge(cols_read, b + 1)
                over_tiles = dmax[:].unsqueeze(1).to_broadcast([P, T, H])
                nc.vector.tensor_tensor(top[:], cols[:, :, 0, :], over_tiles, ALU.add)
                nc.vector.tensor_scalar(clamp[:], dmax[:], -1.0, T_MAX, ALU.mult, ALU.add)
                nc.vector.tensor_tensor(args[:, 0], cols[:, :, 1, :], over_tiles, ALU.subtract).then_inc(top_ready, 1)
                dve.wait_ge(top_ready, b + 1)
                nc.vector.tensor_copy(batch_cols[:, C], clamp[:].unsqueeze(1).to_broadcast([P, T, H]))
                nc.vector.tensor_scalar(args[:, 1], args[:, 0], -RISE, Q_MAX, ALU.mult, ALU.min)
                nc.vector.tensor_scalar(args[:, 2], top[:], T_MAX, RISE, ALU.min, ALU.mult).then_inc(half_args, 1)
                dve.wait_ge(half_args, b + 1)
                nc.vector.tensor_scalar(args[:, 0], args[:, 0], SHIFT, None, ALU.add)
                nc.vector.tensor_scalar(args[:, 1:3], args[:, 1:3], -SHIFT, None, ALU.add).then_inc(args_ready, 1)

            def split_weights(b):
                dve.wait_ge(exps_ready, b + 1)
                nc.vector.tensor_scalar(batch_cols[:, MINUS_Q], batch_cols[:, Q], -1.0, None, ALU.mult)
                nc.vector.tensor_copy(weights[:, 0], batch_cols[:, U])
                nc.vector.tensor_tensor(weights[:, 1], batch_cols[:, U], batch_cols[:, Q],
                                        ALU.mult).then_inc(weights_ready, 1)
                dve.wait_ge(weights_ready, b + 1)
                part = weight_part[:].rearrange("p t h c w -> p c (t h) w")
                left = weights[:].rearrange("p c t h -> p c (t h)")
                nc.vector.tensor_copy(part[:, :, :, 0], left).then_inc(high_part, 1)
                dve.wait_ge(high_part, b + 1)
                nc.vector.tensor_tensor(left, left, part[:, :, :, 0], ALU.subtract).then_inc(weights_rest, 1)
                dve.wait_ge(weights_rest, b + 1)
                nc.vector.tensor_copy(part[:, :, :, 1], left).then_inc(mid_part, 1)
                dve.wait_ge(mid_part, b + 1)
                nc.vector.tensor_tensor(part[:, :, :, 2], left, part[:, :, :, 1], ALU.subtract).then_inc(cols_ready, 1)

            def split_rows(b):
                dve.wait_ge(rows_done, b + 1)
                dve.wait_ge(parts_ready, b + 1)
                dve.wait_ge(turned, b + 1)
                wait_for(dve, src_done, 2 * H * b)
                if isinstance(b, int) and b == 0:
                    dve.wait_ge(part_zero, 1)
                rows = aux_a[0:2 * H]
                hi = row_part[0:2 * H, :].rearrange("p (a n) -> p a n", a=2)
                nc.vector.tensor_copy(hi, rows).then_inc(hi_ready, 1)
                dve.wait_ge(hi_ready, b + 1)
                nc.vector.tensor_tensor(row_rest.rearrange("p (a n) -> p a n", a=2), rows, hi,
                                        ALU.subtract).then_inc(rest_ready, 1)
                dve.wait_ge(rest_ready, b + 1)
                nc.vector.tensor_copy(row_mid, row_rest).then_inc(mid_ready, 1)
                dve.wait_ge(mid_ready, b + 1)
                nc.vector.tensor_tensor(row_part[64:64 + 2 * H, :], row_rest, row_mid,
                                        ALU.subtract).then_inc(rows_ready, 1)

            def take_head(b, h, par):
                m = H * b + h
                dve.wait_ge(cols_ready, b + 1)
                wait_for(dve, sign_used, T * (m - 1))
                nc.vector.tensor_copy(head_part[:, par], weight_part[:, :, bass.ds(h, 1)]
                                      .rearrange("p t o c w -> p t (o c) w"))
                nc.vector.tensor_copy(head_cols[:, par], batch_cols[:, :, :, bass.ds(h, 1)]
                                      .rearrange("p c t o -> p c (t o)")).then_inc(head_ready, 1)

            def values(b, h, par):
                m = H * b + h
                dve.wait_ge(v_done, m + 1)
                dve.wait_ge(head_ready, m + 1)
                for half in range(2):
                    ts = slice(4 * half, 4 * half + 4)
                    last = nc.vector.tensor_tensor(
                        v[:, par, ts, :], aux_a[:, half, :].rearrange("p (t d) -> p t d", d=D),
                        head_cols[:, par, U, ts].unsqueeze(2).to_broadcast([P, 4, D]), ALU.mult)
                last.then_inc(v_ready, 1)

            def tile(m, par, k):
                if k == 0:
                    dve.wait_ge(r_ready, m + 1)
                wait_for(dve, tile_used, T * m + k - RING + 1)
                nc.vector.scalar_tensor_tensor(tiles[:, k % RING, :], r_row[:, par, :], head_cols[:, par, Q, k:k + 1],
                                               g.mask_gt[:, k, :], ALU.max, ALU.mult).then_inc(tile_ready, 1)

            def finish(b, h, par):
                m = H * b + h
                dve.wait_ge(sign_used, T * (m + 1))
                if isinstance(h, int) and h == 0:
                    nc.vector.tensor_reduce(totals[:].rearrange("p h c -> p (h c)"),
                                            totals_ps.rearrange("p (t w) -> p t w", w=3), AX_X,
                                            ALU.add).then_inc(totals_read, 1)
                    dve.wait_ge(totals_read, b + 1)
                nc.vector.tensor_copy(total[:], totals[:, bass.ds(h, 1), :].rearrange("p o c -> p (o c)"))
                nc.vector.tensor_reduce(sums[:].rearrange("p t c -> p (t c)"),
                                        sums_ps.rearrange("p (t w) -> p t w", w=3), AX_X, ALU.add).then_inc(sums_read, 1)
                dve.wait_ge(sums_read, m + 1)
                nc.vector.scalar_tensor_tensor(high[:], sums[:, :, 0], total[:, 0:1], head_cols[:, par, R, :],
                                               ALU.add, ALU.mult).then_inc(high_ready, 1)
                dve.wait_ge(high_ready, m + 1)
                nc.vector.scalar_tensor_tensor(minus_den[:], sums[:, :, 1], total[:, 1:2], high[:],
                                               ALU.subtract, ALU.subtract).then_inc(den_ready, 1)
                dve.wait_ge(den_ready, m + 1)
                nc.vector.reciprocal(recip[:], minus_den[:]).then_inc(recip_ready, 1)
                dve.wait_ge(recip_ready, m + 1)
                nc.vector.tensor_scalar(scale[:], recip[:], -2.0, None, ALU.mult).then_inc(scale_ready, 1)
                dve.wait_ge(scale_ready, m + 1)
                dve.wait_ge(tile_used, T * (m + 1))
                dve.wait_ge(offv_read, m + 1)
                if not isinstance(m, int) or m >= 2:
                    dve.wait_ge(x_done, m)
                for it in range(T):
                    last = nc.vector.scalar_tensor_tensor(
                        z[:, par, it, :], ps[:, 2 * par + it // 4, (it % 4) * D:(it % 4 + 1) * D],
                        scale[:, it:it + 1], off[:, par, it, :], ALU.mult, ALU.add)
                last.then_inc(z_ready, 1)

            def step(b, h, par, first=False, last=False, shared=False):
                m = H * b + h
                b1, h1 = following(b, h)
                for k in range(T):
                    tile(m, par, k)
                    if k == 0 and shared and par == 0:
                        moments(b + 1)
                    if k == 1 and shared and par == 0:
                        norm(b + 1)
                    if k == 1 and last:
                        dve.wait_ge(x_done, H + 1)
                        layer_moments(nc, g, s, dve, next_layer, 0)
                    if k == 2 and shared and par == 1:
                        read_cols(b + 1)
                    if k == 3:
                        if not first:
                            finish(*before(b, h), 1 - par)
                        if shared and par == 1:
                            exponents(b + 1)
                        elif not last:
                            take_head(b1, h1, 1 - par)
                    if k == 4 and shared and par == 1:
                        split_rows(b + 1)
                    if k == 5 and shared and par == 1:
                        split_weights(b + 1)
                        take_head(b1, h1, 1 - par)
                    if k == (7 if shared and par == 1 else 5) and not last:
                        values(b1, h1, 1 - par)

            nc.vector.tensor_scalar(mask_off[:], g.mask_gt[:], -1.0, 1.0, ALU.mult, ALU.add).then_inc(off_mask_ready, 1)
            read_cols(0)
            exponents(0)
            split_rows(0)
            split_weights(0)
            take_head(0, 0, 0)
            values(0, 0, 0)
            all_maps(dve, step)
            finish(B - 1, H - 1, 1)

        @block.scalar
        def _(act):
            def relu_h(b):
                act.wait_ge(turned, b + 1)
                wait_for(act, v_done, H * b)
                nc.scalar.activation(h_t[:].rearrange("p (a n) -> p a n", a=2), aux_a, ACT.Relu).then_inc(h_ready, 1)

            def exps(b):
                act.wait_ge(args_ready, b + 1)
                wait_for(act, head_ready, H * b)
                nc.scalar.activation(batch_cols[:, U:R + 1], args[:], ACT.Exp).then_inc(exps_ready, 1)

            def move_mid(b):
                act.wait_ge(mid_ready, b + 1)
                wait_for(act, src_done, 2 * H * b)
                if isinstance(b, int) and b == 0:
                    act.wait_ge(part_zero, 1)
                nc.scalar.activation(row_part[32:32 + 2 * H, :], row_mid, ACT.Copy).then_inc(mid_moved, 1)

            def off_rows(b, half):
                act.wait_ge(off_done, 2 * b + half + 1)
                wait_for(act, offv_done, H * b)
                nc.scalar.activation(off_t[:, half * HALF:(half + 1) * HALF], aux_b, ACT.Copy,
                                     scale=NEG_BIG).then_inc(off_ready, 1)

            def source(m, par, half):
                act.wait_ge(head_ready, m + 1)
                act.wait_ge(src_done, 2 * m + half + 1)
                wait_for(act, tile_ready, T * (m - 1))
                nc.scalar.activation(r_row[:, par, half * HALF:(half + 1) * HALF], aux_b, ACT.Relu,
                                     bias=head_cols[:, par, C, 0:1], scale=-1.0).then_inc(src_read, 1)

            def r_exp(m, par):
                act.wait_ge(src_read, 2 * m + 2)
                nc.scalar.activation(r_row[:, par, :], r_row[:, par, :], ACT.Exp, bias=g.bias_r[:],
                                     scale=-RISE).then_inc(r_ready, 1)

            def off_values(m, par):
                act.wait_ge(offv_done, m + 1)
                wait_for(act, z_ready, m - 1)
                nc.scalar.activation(off[:, par].rearrange("p (a t) d -> p a (t d)", a=2), aux_a,
                                     ACT.Copy).then_inc(offv_read, 1)

            def signs(m, par, k):
                if k == 0:
                    act.wait_ge(r_ready, m + 1)
                wait_for(act, sign_used, T * (m - 1) + k + 1)
                nc.scalar.activation(sign[:, k, :], r_row[:, par, :], ACT.Sign,
                                     bias=head_cols[:, par, MINUS_Q, k:k + 1]).then_inc(sign_ready, 1)

            def tanh(m, par):
                act.wait_ge(z_ready, m + 1)
                nc.scalar.activation(z[:, par], z[:, par], ACT.Tanh, scale=0.5).then_inc(tanh_ready, 1)

            def step(b, h, par, first=False, last=False, shared=False):
                m = H * b + h
                last_head = shared and par == 1
                for k in range(T):
                    signs(m, par, k)
                    if last_head:
                        if k == 1:
                            off_rows(b + 1, 0)
                        if k == 2:
                            exps(b + 1)
                        if k == 3:
                            off_rows(b + 1, 1)
                            move_mid(b + 1)
                    if not last:
                        if k == (5 if last_head else 2):
                            source(m + 1, 1 - par, 0)
                        if k == (6 if last_head else 3):
                            source(m + 1, 1 - par, 1)
                            r_exp(m + 1, 1 - par)
                        if k == (7 if last_head else 5):
                            off_values(m + 1, 1 - par)
                    if k == (7 if last_head else 4) and not first:
                        tanh(m - 1, 1 - par)
                if shared and par == 0:
                    relu_h(b + 1)
                if last:
                    act.wait_ge(turned, B)
                    act.wait_ge(relu_ready, B)
                    act.wait_ge(rows_ready, B)
                    layer_norm(nc, g, s, act, next_layer, 0)

            relu_h(0)
            exps(0)
            move_mid(0)
            off_rows(0, 0)
            off_rows(0, 1)
            source(0, 0, 0)
            source(0, 0, 1)
            r_exp(0, 0)
            off_values(0, 0)
            all_maps(act, step)
            tanh(B * H - 1, 1)

        @block.gpsimd
        def _(pool):
            def split_h(b):
                wait_alone(pool, g.pool_passed, normed, b)
                wait_alone(pool, g.pool_passed, off_done, 2 * b)
                wait_alone(pool, g.pool_passed, rows_ready, b)
                nc.gpsimd.tensor_scalar(h_part[:, 0], hn[:], 0.0, None, ALU.max)
                nc.gpsimd.tensor_scalar(h_rest[:], hn[:], 0.0, None, ALU.max).then_inc(relu_ready, 1)
                wait_alone(pool, g.pool_passed, relu_ready, b + 1)
                nc.gpsimd.tensor_tensor(h_rest[:], h_rest[:], h_part[:, 0], ALU.subtract).then_inc(rest1, 1)
                wait_alone(pool, g.pool_passed, rest1, b + 1)
                nc.gpsimd.tensor_copy(h_part[:, 1], h_rest[:]).then_inc(part1, 1)
                wait_alone(pool, g.pool_passed, part1, b + 1)
                nc.gpsimd.tensor_tensor(h_part[:, 2], h_rest[:], h_part[:, 1], ALU.subtract).then_inc(parts_ready, 1)

            def add_base(b):
                nc.gpsimd.tensor_tensor(g.x[:, b], g.x[:, b], g.base1[:].unsqueeze(2).to_broadcast([P, T, D]), ALU.add).then_inc(base_added, 1)

            def inverse_root(b):
                wait_alone(pool, g.pool_passed, var_ready, b)
                nc.gpsimd.tensor_tensor(rstd[:], var_eps[:], g.minus_half[:], ALU.pow).then_inc(rstd_done, 1)

            def reduce_max(b):
                wait_alone(pool, g.pool_passed, cols_read, b + 1)
                nc.gpsimd.partition_all_reduce(dmax[:], dmax1[:], P, REDUCE_MAX).then_inc(dmax_ready, 1)

            def weigh(b, h, m, par):
                wait_alone(pool, g.pool_passed, tanh_ready, m + 1)
                nc.gpsimd.tensor_tensor(z[:, par], z[:, par],
                                        g.half_w[:, bass.ds(h, 1)].unsqueeze(2).to_broadcast([P, T, D]), ALU.mult).then_inc(weighed, 1)
                wait_alone(pool, g.pool_passed, weighed, m + 1)
                wait_alone(pool, g.pool_passed, base_added, b + 1)
                wait_alone(pool, g.pool_passed, x_done, m + 1)
                nc.gpsimd.tensor_tensor(g.x[:, b], g.x[:, b], z[:, par], ALU.add).then_inc(x_done, 1)

            def step(b, h, par, first=False, last=False, shared=False):
                m = H * b + h
                if shared and par == 0:
                    inverse_root(b + 1)
                    split_h(b + 1)
                if last:
                    layer_inverse_root(nc, g, s, pool, next_layer, 0)
                if not first:
                    weigh(*before(b, h), m - 1, 1 - par)
                if shared and par == 0:
                    add_base(b + 1)
                    reduce_max(b + 1)

            nc.gpsimd.memset(ones[:], 1.0).then_inc(ones_ready, 1)
            nc.gpsimd.memset(row_part[:], 0.0).then_inc(part_zero, 1)
            pool.sem_inc(x_done, 1)
            split_h(0)
            add_base(0)
            reduce_max(0)
            all_maps(pool, step)
            weigh(B - 1, H - 1, B * H - 1, 1)

        @block.tensor
        def _(pe):
            def turn(b):
                wait_for(pe, normed, b)
                wait_for(pe, offv_read, H * b)
                for it in range(T):
                    last = nc.tensor.transpose(aux_a[:, it // 4, (it % 4) * P:(it % 4 + 1) * P], hn[:, it, :],
                                               g.ident[:])
                last.then_inc(turned, 1)

            def score_cols(b):
                pe.wait_ge(h_ready, b + 1)
                wait_for(pe, src_read, 2 * H * b)
                for jt in range(T):
                    last = nc.tensor.matmul(aux_b[:, 2 * H * jt:2 * H * (jt + 1)], h_t[:, jt * P:(jt + 1) * P],
                                            g.wa_heads[:].rearrange("p c h -> p (c h)"), start=True, stop=True)
                last.then_inc(cols_done, 1)

            def score_rows(b):
                pe.wait_ge(h_ready, b + 1)
                for half in range(2):
                    last = nc.tensor.matmul(aux_a[0:2 * H, half, :], g.wa_heads[:].rearrange("p c h -> p (c h)"),
                                            h_t[:, half * HALF:(half + 1) * HALF], start=True, stop=True)
                last.then_inc(rows_done, 1)

            def off_sums(b, half):
                if half == 0:
                    pe.wait_ge(parts_ready, b + 1)
                    pe.wait_ge(off_mask_ready, 1)
                    pe.wait_ge(cols_read, b + 1)
                else:
                    pe.wait_ge(off_ready, 2 * b + 1)
                for jt in range(T):
                    for part in range(3):
                        last = nc.tensor.matmul(aux_b, h_part[:, part, jt, :],
                                                mask_off[:, jt, half * HALF:(half + 1) * HALF],
                                                start=(jt == 0 and part == 0), stop=(jt == T - 1 and part == 2))
                last.then_inc(off_done, 1)

            def source(b, h, m, half, new_batch):
                if half == 1:
                    pe.wait_ge(src_read, 2 * m + 1)
                elif new_batch:
                    pe.wait_ge(off_ready, 2 * b + 2)
                    pe.wait_ge(rows_ready, b + 1)
                    pe.wait_ge(mid_moved, b + 1)
                else:
                    pe.wait_ge(src_read, 2 * m)
                nc.tensor.matmul(aux_b, g.sel[0:96, bass.ds(h, 1), :].rearrange("k o p -> k (o p)"),
                                 row_part[:, half * HALF:(half + 1) * HALF], start=True,
                                 stop=True).then_inc(src_done, 1)

            def values(b, h, m, new_batch):
                if new_batch:
                    pe.wait_ge(rest_ready, b + 1)
                else:
                    pe.wait_ge(offv_read, m)
                wh = g.w_in[:, bass.ds(h + W_HEADS, 1), :].rearrange("p o d -> p (o d)")
                for jt in range(T):
                    last = nc.tensor.matmul(aux_a[:, jt // 4, (jt % 4) * D:(jt % 4 + 1) * D],
                                            h_t[:, jt * P:(jt + 1) * P], wh, start=True, stop=True)
                last.then_inc(v_done, 1)

            def off_values(b, h, m):
                pe.wait_ge(v_ready, m + 1)
                wh = g.w_in[:, bass.ds(h + W_HEADS, 1), :].rearrange("p o d -> p (o d)")
                for it in range(T):
                    last = nc.tensor.matmul(aux_a[:, it // 4, (it % 4) * D:(it % 4 + 1) * D],
                                            off_t[:, it * P:(it + 1) * P], wh, start=True, stop=True)
                last.then_inc(offv_done, 1)

            def sign_sums(h, m, par, k):
                new_batch = isinstance(h, int) and h == 0
                if k == 0:
                    pe.wait_ge(head_ready, m + 1)
                    wait_for(pe, sums_read, m)
                    if new_batch:
                        if isinstance(m, int) and m == 0:
                            pe.wait_ge(ones_ready, 1)
                        for jt in range(T):
                            nc.tensor.matmul(totals_ps, ones[:], weight_part[:, jt].rearrange("p h c w -> p (h c w)"),
                                             start=(jt == 0), stop=(jt == T - 1), skip_group_check=True)
                pe.wait_ge(sign_ready, T * m + k + 1)
                for it in range(T):
                    last = nc.tensor.matmul(sums_ps[:, 6 * it:6 * it + 6], sign[:, k, it * P:(it + 1) * P],
                                            head_part[:, par, k].rearrange("p c w -> p (c w)"),
                                            start=(k == 0 and it == 0 and not new_batch), stop=(k == T - 1),
                                            skip_group_check=True)
                last.then_inc(sign_used, 1)

            def products(m, par, k):
                if k == 0:
                    pe.wait_ge(v_ready, m + 1)
                    wait_for(pe, z_ready, m - 1)
                pe.wait_ge(tile_ready, T * m + k + 1)
                for it in range(T):
                    last = nc.tensor.matmul(ps[:, 2 * par + it // 4, (it % 4) * D:(it % 4 + 1) * D],
                                            tiles[:, k % RING, it * P:(it + 1) * P], v[:, par, k, :],
                                            start=(k == 0 and it % 4 == 0), stop=(k == T - 1), skip_group_check=True)
                last.then_inc(tile_used, 1)

            def step(b, h, par, first=False, last=False, shared=False):
                m = H * b + h
                b1, h1 = following(b, h)
                last_head = shared and par == 1
                for k in range(T):
                    products(m, par, k)
                    if last_head:
                        if k == 0:
                            score_rows(b + 1)
                        if k == 1:
                            off_sums(b + 1, 0)
                        if k == 2:
                            off_sums(b + 1, 1)
                    if not last:
                        if k == (5 if last_head else 2):
                            source(b1, h1, m + 1, 0, last_head)
                            values(b1, h1, m + 1, last_head)
                        if k == (6 if last_head else 3):
                            source(b1, h1, m + 1, 1, last_head)
                        if k == (7 if last_head else 4):
                            off_values(b1, h1, m + 1)
                    if k % 4 == 3:
                        for j in range(k - 3, k + 1):
                            sign_sums(h, m, par, j)
                    if shared and par == 0:
                        if k == 6:
                            turn(b + 1)
                        if k == 7:
                            score_cols(b + 1)

            turn(0)
            score_cols(0)
            score_rows(0)
            off_sums(0, 0)
            off_sums(0, 1)
            source(0, 0, 0, 0, True)
            source(0, 0, 0, 1, True)
            values(0, 0, 0, True)
            off_values(0, 0, 0)
            all_maps(pe, step)


def gat_stack(nc, x_h, adj_h, w_in_h, w_out_h, a_h, avg_w_h, avg_b_h, out_h):
    with ExitStack() as ctx:
        def sb(name, shape, dt=FP32):
            return ctx.enter_context(nc.sbuf_tensor(name, shape, dt))

        g = Shared()
        g.x = sb("x_all", [P, B, T, D])
        g.mask_gt = sb("mask_gt", [P, T, N], BF16)
        g.mask_ne = sb("mask_ne", [P, T, N], UINT8)
        g.w_in = sb("w_in", [P, W_HEADS + H, D])
        g.wa = sb("wa", [P, W_HEADS + H, 2])
        g.wa_heads = sb("wa_heads", [P, 2, H])
        g.ident = sb("ident", [P, P])
        g.sel = sb("sel", [P, H, P], BF16)
        g.empty_gt, g.empty_ne = sb("empty_gt", [P, T]), sb("empty_ne", [P, T])
        g.avg_w, g.avg_b = sb("avg_w", [P, H]), sb("avg_b", [P, 1])
        g.half_w, g.half_sum, g.base1 = sb("half_w", [P, H]), sb("half_sum", [P, 1]), sb("base1", [P, 1])
        g.minus_half = sb("minus_half", [P, T])
        g.stats, g.mom = sb("stats", [P, T, 6]), sb("mom", [P, T, 2])
        g.var_eps, g.rstd = sb("var_eps", [P, T]), sb("rstd", [P, T])
        g.minus_mean, g.shift = sb("minus_mean", [P, T]), sb("shift", [P, T])
        g.h = sb("h", [P, T, D])
        g.bias_up, g.bias_down, g.bias_r = sb("bias_up", [P, 1]), sb("bias_down", [P, 1]), sb("bias_r", [P, 1])

        g.pool_passed = ctx.enter_context(nc.semaphore("pool_passed"))
        g.dve_passed = ctx.enter_context(nc.semaphore("dve_passed"))
        g.x_first, g.x_rest = ctx.enter_context(nc.semaphore("x_first")), ctx.enter_context(nc.semaphore("x_rest"))

        setup(nc, g, (x_h, adj_h, w_in_h, w_out_h, a_h, avg_w_h, avg_b_h))
        s = masked_semaphores(nc, ctx)
        layer0, layer1, layer2, layer3 = (MaskedLayer(g, 0, 0), HeadLayer(), MaskedLayer(g, 2, 1),
                                          MaskedLayer(g, 3, 2))
        masked_layers(nc, g, s, [layer0], False, layer1, None)
        head_layer(nc, g, s, layer2)
        masked_layers(nc, g, s, [layer2, layer3], True, None, out_h)


def kernel(x, adj, L0_gnn_W, L0_gnn_a, L1_gnn_W, L1_gnn_a, L1_gnn_avg_w, L1_gnn_avg_b, L2_gnn_W, L2_gnn_a,
           L3_gnn_W, L3_gnn_a):
    import numpy as np
    import concourse.bacc as bacc
    from concourse.bass_utils import run_bass_kernel_spmd

    w0, w1, w2, w3 = (np.asarray(w) for w in (L0_gnn_W, L1_gnn_W, L2_gnn_W, L3_gnn_W))
    w_in = np.concatenate([w0[:, None], w2.T[:, None], w3.T[:, None], w1.transpose(1, 0, 2)], axis=1)
    w_out = np.concatenate([w0.T[:, None], w2[:, None], w3[:, None], w1.transpose(2, 0, 1)], axis=1)
    a = np.stack([np.asarray(v).reshape(2, 128).T for v in (L0_gnn_a, L2_gnn_a, L3_gnn_a)]
                 + [np.asarray(L1_gnn_a)[h].reshape(2, 128).T for h in range(8)], axis=1)
    arrays = {
        "x_in": np.asarray(x), "adj_in": np.asarray(adj), "w_in_in": w_in, "w_out_in": w_out, "a_in": a,
        "avg_w_in": np.broadcast_to(np.asarray(L1_gnn_avg_w).reshape(1, 8), (128, 8)),
        "avg_b_in": np.broadcast_to(np.asarray(L1_gnn_avg_b).reshape(1, 1), (128, 1)),
    }
    arrays = {k: np.ascontiguousarray(v) for k, v in arrays.items()}
    nc = bacc.Bacc("TRN2", target_bir_lowering=False, num_devices=1)
    aps = [nc.dram_tensor(k, v.shape, mybir.dt.from_np(v.dtype), kind="ExternalInput").ap() for k, v in arrays.items()]
    out = nc.dram_tensor("out", (16, 1024, 128), FP32, kind="ExternalOutput").ap()
    gat_stack(nc, *aps, out)
    r = run_bass_kernel_spmd(nc, [arrays], core_ids=[0])
    return r.results[0]["out"]
```

```python
from contextlib import ExitStack

import concourse.bass as bass
from concourse import mybir

FP32 = mybir.dt.float32
BF16 = mybir.dt.bfloat16
INT32 = mybir.dt.int32
UINT8 = mybir.dt.uint8
ALU = mybir.AluOpType
ACT = mybir.ActivationFunctionType
AX_X = mybir.AxisListType.X
REDUCE_MAX = bass.bass_isa.ReduceOp.max

B = 16
N = 1024
D = 128
P = 128
T = N // P
H = 8
HALF = 512
RING = 4
EPS = 1e-5
SLOPE = 0.2
NEG_BIG = -9.0e15

RISE = 1.0 - SLOPE
SHIFT = 20.0
T_MAX = 93.0
Q_MAX = 105.0

W_ROW = {0: 0, 2: 1, 3: 2}
W_HEADS = 3


def wait_for(eng, sem, value):
    if isinstance(value, int) and value <= 0:
        return
    eng.wait_ge(sem, value)


def wait_alone(eng, passed, sem, value):
    wait_for(eng, sem, value)
    if not isinstance(value, int):
        eng.sem_inc(passed, 1)


class Shared:
    pass


def setup(nc, g, s, first_layer, ins):
    x_h, adj_h, w_in_h, w_out_h, a_h, avg_w_h, avg_b_h = ins
    with ExitStack() as ctx:
        def sb(name, shape, dt):
            return ctx.enter_context(nc.sbuf_tensor(name, shape, dt))

        def sem(name):
            return ctx.enter_context(nc.semaphore(name))

        adj_rows = sb("adj_rows", [P, T, N], INT32)
        mask_rows = sb("mask_rows", [P, 2, 2, N], BF16)
        w_out = sb("w_out", [P, W_HEADS + H, D], FP32)
        a_cols = sb("a_cols", [P, W_HEADS + H, 2], FP32)
        row_count = sb("row_count", [P, 2, T], FP32)
        counted = sb("counted", [P, 4, N], BF16)
        ident_bf = sb("ident_bf", [P, P], BF16)
        mask_ps = ctx.enter_context(nc.psum_tensor("mask_ps", [P, 4, N], BF16))
        wa_ps = ctx.enter_context(nc.psum_tensor("wa_ps", [P, HALF], FP32))

        adj_in = [sem(f"adj_in{i}") for i in range(T)]
        w_loaded, minus_half_set = sem("w_loaded"), sem("minus_half_set")
        ident_zero, ident_made = sem("ident_zero"), sem("ident_made")
        sel_zero, sel_made = sem("sel_zero"), sem("sel_made")
        masks_made, masks_turned, mask1_copied, mask3_copied = (
            sem("masks_made"), sem("masks_turned"), sem("mask1_copied"), sem("mask3_copied"))
        wa_done, wa_copied = sem("wa_done"), sem("wa_copied")
        rows_counted, ident_bf_made = sem("rows_counted"), sem("ident_bf_made")

        block = ctx.enter_context(nc.Block())

        def load_x(eng, lo, hi, loaded):
            eng.dma_start(g.x[:, lo:hi], x_h[lo:hi].rearrange("b (t p) d -> p b t d", p=P)).then_inc(loaded, 16)

        @block.sync
        def _(sp):
            for it in range(T):
                sp.dma_start(adj_rows[:, it, :], adj_h[it * P:(it + 1) * P, :]).then_inc(adj_in[it], 16)
                if it == 3:
                    load_x(sp, 0, 1, g.x_in[0])
            load_x(sp, 1, 4, g.x_in[1])
            for b in range(4, B, 4):
                load_x(sp, b, b + 4, g.x_in[2])

        @block.scalar
        def _(act):
            act.dma_start(w_out[:], w_out_h).then_inc(w_loaded, 16)
            act.dma_start(a_cols[:], a_h).then_inc(w_loaded, 16)
            act.dma_start(g.w_wide[:, :, 0:D], w_in_h[:, 0:W_HEADS, :]).then_inc(w_loaded, 16)
            act.dma_start(g.w_heads[:], w_in_h[:, W_HEADS:, :]).then_inc(w_loaded, 16)
            act.dma_start(g.avg_w[:], avg_w_h).then_inc(w_loaded, 16)
            act.dma_start(g.avg_b[:], avg_b_h).then_inc(w_loaded, 16)
            for it in range(T):
                act.wait_ge(masks_made, it + 1)
                for kind in range(2):
                    if it >= 2:
                        act.wait_ge(rows_counted, 2 * it + kind - 3)
                    nc.scalar.activation(counted[:, (2 * it + kind) % 4], mask_rows[:, it % 2, kind, :], ACT.Copy,
                                         accum_out=row_count[:, kind, it:it + 1]).then_inc(rows_counted, 1)
                act.wait_ge(masks_turned, 2 * it + 1)
                nc.scalar.activation(g.mask_gt[:, :, it * P:(it + 1) * P],
                                     mask_ps[:, (2 * it) % 4, :].rearrange("p (t i) -> p t i", t=T),
                                     ACT.Copy).then_inc(mask1_copied, 1)
            layer_norm(nc, g, s, act, first_layer, 0)

        @block.gpsimd
        def _(pool):
            nc.gpsimd.memset(g.ident[:], 0.0).then_inc(ident_zero, 1)
            pool.wait_ge(ident_zero, 1)
            nc.gpsimd.affine_select(out=g.ident[:], in_=g.ident[:], compare_op=ALU.not_equal, fill=1.0, base=0,
                                    pattern=[[-1, P]], channel_multiplier=1).then_inc(ident_made, 1)
            nc.gpsimd.memset(g.sel[:], 0.0).then_inc(sel_zero, 1)
            pool.wait_ge(sel_zero, 1)
            for part in range(3):
                nc.gpsimd.affine_select(out=g.sel[:], in_=g.sel[:], compare_op=ALU.not_equal, fill=1.0,
                                        base=-32 * part, pattern=[[-1, H], [0, P]],
                                        channel_multiplier=1).then_inc(sel_made, 1)
                pool.wait_ge(sel_made, part + 1)
            nc.gpsimd.memset(g.minus_half[:], -0.5).then_inc(minus_half_set, 1)
            nc.gpsimd.memset(g.bias_up[:], SHIFT)
            nc.gpsimd.memset(g.bias_down[:], -SHIFT)
            nc.gpsimd.memset(g.bias_r[:], RISE * T_MAX - SHIFT)
            pool.wait_ge(minus_half_set, 1)
            layer_inverse_root(nc, g, s, pool, first_layer, 0)

        def copy_mask3(dve, it):
            dve.wait_ge(masks_turned, 2 * it + 2)
            nc.vector.tensor_copy(g.mask_ne[:, :, it * P:(it + 1) * P],
                                  mask_ps[:, (2 * it + 1) % 4, :].rearrange("p (t i) -> p t i", t=T)
                                  ).then_inc(mask3_copied, 1)

        @block.vector
        def _(dve):
            dve.wait_ge(ident_made, 1)
            nc.vector.tensor_copy(ident_bf[:], g.ident[:]).then_inc(ident_bf_made, 1)
            for it in range(T):
                dve.wait_ge(adj_in[it], 16)
                if it >= 2:
                    dve.wait_ge(masks_turned, 2 * (it - 1))
                    dve.wait_ge(rows_counted, 2 * (it - 1))
                rows = adj_rows[:, it, :]
                nc.vector.tensor_scalar(mask_rows[:, it % 2, 0, :], rows, 0.0, None, ALU.is_gt)
                nc.vector.tensor_scalar(mask_rows[:, it % 2, 1, :], rows, 0.0, None,
                                        ALU.not_equal).then_inc(masks_made, 1)
                if it >= 1:
                    copy_mask3(dve, it - 1)
                if it == T - 2:
                    layer_moments(nc, g, s, dve, first_layer, 0)
            copy_mask3(dve, T - 1)
            dve.wait_ge(rows_counted, 2 * T)
            nc.vector.tensor_scalar(g.empty_gt[:], row_count[:, 0, :], 0.0, None, ALU.is_le)
            nc.vector.tensor_scalar(g.empty_ne[:], row_count[:, 1, :], 0.0, None, ALU.is_le)
            dve.wait_ge(wa_done, 1)
            nc.vector.tensor_copy(g.w_wide[:, :, D:], wa_ps[:, 0:2 * W_HEADS].rearrange("p (l t) -> p l t", t=2))
            nc.vector.tensor_copy(g.wa_heads[:], wa_ps[:, 2 * W_HEADS:2 * (W_HEADS + H)]
                                  .rearrange("p (h t) -> p t h", t=2)).then_inc(wa_copied, 1)
            dve.wait_ge(wa_copied, 1)
            dve.wait_ge(w_loaded, 96)
            nc.vector.tensor_scalar(g.half_w[:], g.avg_w[:], 0.5, None, ALU.mult).then_inc(wa_copied, 1)
            dve.wait_ge(wa_copied, 2)
            nc.vector.tensor_reduce(g.half_sum[:], g.half_w[:], AX_X, ALU.add).then_inc(wa_copied, 1)
            dve.wait_ge(wa_copied, 3)
            nc.vector.tensor_tensor(g.base1[:], g.half_sum[:], g.avg_b[:], ALU.add)

        @block.tensor
        def _(pe):
            pe.wait_ge(ident_bf_made, 1)
            for it in range(T):
                pe.wait_ge(masks_made, it + 1)
                for kind in range(2):
                    if it >= 2:
                        pe.wait_ge((mask1_copied, mask3_copied)[kind], it - 1)
                    for jt in range(T):
                        last = nc.tensor.transpose(mask_ps[:, (2 * it + kind) % 4, jt * P:(jt + 1) * P],
                                                   mask_rows[:, it % 2, kind, jt * P:(jt + 1) * P], ident_bf[:])
                    last.then_inc(masks_turned, 1)
            pe.wait_ge(w_loaded, 96)
            for row in range(W_HEADS + H):
                last = nc.tensor.matmul(wa_ps[:, 2 * row:2 * row + 2], w_out[:, row, :], a_cols[:, row, :],
                                        start=True, stop=True)
            last.then_inc(wa_done, 1)


def masked_semaphores(nc, ctx):
    names = ["stats", "moments", "var_ready", "rstd", "shift_ready", "h_ready", "turned", "ht_ready", "cols_copied",
             "cols_read", "dmax_ready", "drop_ready", "args_ready", "u_ready", "q_ready", "r_col_ready", "row_done",
             "r_ready", "v_done", "v_ready", "tile_ready", "tile_used", "bank_done", "empty_ready", "addend_ready",
             "den_ready", "recip_ready", "acc_read", "low_ready", "elu_exp", "elu_less", "x_done"]
    return {n: ctx.enter_context(nc.semaphore("m_" + n)) for n in names}


class MaskedLayer:

    def __init__(self, g, layer, order):
        self.mask = g.mask_ne if layer == 3 else g.mask_gt
        self.empty = g.empty_ne if layer == 3 else g.empty_gt
        self.elu = layer == 2
        self.after_elu = layer == 3
        self.loads_x = layer == 0
        self.w = g.w_wide[:, W_ROW[layer], :]
        self.done = B * order
        self.normed = B * order + (1 if layer >= 2 else 0)
        self.addends = {0: 0, 2: B, 3: B}[layer]
        self.before = self.after = None
        self.early = None


class HeadLayer:
    after_elu = loads_x = False
    done = normed = B


def layer_moments(nc, g, s, dve, la, b):
    n = la.normed + b
    if isinstance(b, int) and la.loads_x and b < 4:
        dve.wait_ge(g.x_in[min(b, 1)], 16)
        if b == 3:
            dve.wait_ge(g.x_in[2], 16 * (B - 4) // 4)
    if la.after_elu:
        wait_for(dve, s["x_done"], b + 1)
    wait_for(dve, s["shift_ready"], n)
    for it in range(T):
        last = nc.vector.bn_stats(g.stats[:, it, :], g.x[:, b, it, :])
    last.then_inc(s["stats"], 1)
    wait_alone(dve, g.dve_passed, s["stats"], n + 1)
    for it in range(T):
        last = nc.vector.bn_aggr(g.mom[:, it, :], g.stats[:, it, :])
    last.then_inc(s["moments"], 1)
    dve.wait_ge(s["moments"], n + 1)
    nc.vector.tensor_scalar(g.minus_mean[:], g.mom[:, :, 0], -1.0, None, ALU.mult)
    nc.vector.tensor_scalar(g.var_eps[:], g.mom[:, :, 1], EPS, None, ALU.add).then_inc(s["var_ready"], 1)


def layer_inverse_root(nc, g, s, pool, la, b):
    n = la.normed + b
    wait_alone(pool, g.pool_passed, s["var_ready"], n + 1)
    wait_alone(pool, g.pool_passed, s["h_ready"], n)
    nc.gpsimd.tensor_tensor(g.rstd[:], g.var_eps[:], g.minus_half[:], ALU.pow).then_inc(s["rstd"], 1)
    wait_alone(pool, g.pool_passed, s["rstd"], n + 1)
    nc.gpsimd.tensor_tensor(g.shift[:], g.minus_mean[:], g.rstd[:], ALU.mult).then_inc(s["shift_ready"], 1)


def layer_norm(nc, g, s, act, la, b):
    act.wait_ge(s["shift_ready"], la.normed + b + 1)
    wait_for(act, s["turned"], la.done + b)
    for it in range(T):
        last = nc.scalar.activation(g.h[:, it, :], g.x[:, b, it, :], ACT.Relu, bias=g.shift[:, it:it + 1],
                                    scale=g.rstd[:, it:it + 1])
    last.then_inc(s["h_ready"], 1)


def masked_layers(nc, g, s, layers, early, out_h):
    V1 = D + 1
    V2 = D + 2
    BANKS = (T + 2) // 3
    for one, two in zip(layers, layers[1:]):
        one.after, two.before = two, one
    layers[-1].early = early
    any_elu = any(la.elu for la in layers)

    with ExitStack() as ctx:
        def sb(name, shape, dt=FP32):
            return ctx.enter_context(nc.sbuf_tensor(f"{name}_m{layers[0].done}", shape, dt))

        h = g.h
        h_t = sb("h_t", [P, 2, N])
        h_sum = sb("h_sum", [P, 2])
        cols = sb("cols", [P, 2, T, 2])
        mean_v = sb("mean_v", [P, 2, D])
        dmax1, dmax = sb("dmax1", [P, 1]), sb("dmax", [P, 2])
        drop, rise, top = sb("drop", [P, 2, T]), sb("rise", [P, 2, T]), sb("top", [P, 2, T])
        q, r_col = sb("q", [P, 2, T]), sb("r_col", [P, 2, T])
        r_row = sb("r_row", [P, 2, N])
        v = sb("v", [P, 2, T, V1])
        tiles = sb("tiles", [P, RING, N])
        spread = sb("spread", [P, T, D])
        addend = sb("addend", [P, 2, T, D])
        den, recip = sb("den", [P, T]), sb("recip", [P, T])
        if any_elu:
            y, low, ex = sb("y", [P, T, D]), sb("low", [P, T, D]), sb("ex", [P, T, D])
        ps = ctx.enter_context(nc.psum_tensor(f"ps_m{layers[0].done}", [P, 8, HALF], FP32))
        turns = ps[:, 6:8, :]
        out_done = ctx.enter_context(nc.semaphore(f"out_done{layers[0].done}"))

        def acc(it, lo, hi):
            at = (it % 3) * V1
            return ps[:, it // 3, at + lo:at + hi]

        def val(jt, lo, hi):
            at = (jt % 3) * V2
            return ps[:, BANKS + jt // 3, at + lo:at + hi]

        mean_at = 2 * V2
        mean_ps = ps[:, BANKS + 2, mean_at:mean_at + D]

        def halves(ap):
            return ap.rearrange("p (a n) -> p a n", a=2)

        def moved(la, b, by):
            if isinstance(b, int) and not 0 <= b + by < B:
                other = la.after if by > 0 else la.before
                return other and (other, (b + by) % B)
            return la, b + by

        def steps(eng, step):
            for la in layers:
                step(la, 0, 0)
                step(la, 1, 1)
                with eng.Fori(0, (B - 4) // 2) as j:
                    step(la, 2 * j + 2, 0)
                    step(la, 2 * j + 3, 1)
                step(la, B - 2, 0)
                step(la, B - 1, 1)

        def begin(f, by):
            def call(la, b, par):
                at = moved(la, b, by)
                if at:
                    f(*at, (par + by) % 2)
            return call

        def norming(f, eng):
            def call(la, b, par):
                at = moved(la, b, 2)
                if not at and la.early and b == B - 2:
                    at = (la.early, 0)
                if at:
                    f(nc, g, s, eng, *at)
            return call

        block = ctx.enter_context(nc.Block())
        first = layers[0]

        @block.vector
        def _(dve):
            def read_cols(la, b, par):
                n = la.done + b
                dve.wait_ge(s["v_done"], n + 1)
                wait_for(dve, s["empty_ready"], n - 1)
                nc.vector.tensor_copy(cols[:, par, 0:6, :].rearrange("p (a t) c -> p a t c", a=2),
                                      ps[:, BANKS:BANKS + 2, 0:3 * V2].rearrange("p a (t c) -> p a t c", c=V2)
                                      [:, :, :, D:V2])
                nc.vector.tensor_copy(cols[:, par, 6:T, :], ps[:, BANKS + 2, 0:2 * V2]
                                      .rearrange("p (t c) -> p t c", c=V2)[:, :, D:V2]).then_inc(s["cols_copied"], 1)
                nc.vector.tensor_scalar(mean_v[:, par, :], mean_ps, 1.0 / N, None, ALU.mult)
                dve.wait_ge(s["cols_copied"], n + 1)
                nc.vector.tensor_reduce(dmax1[:], cols[:, par].rearrange("p t c -> p c t")[:, 1, :],
                                        AX_X, ALU.max).then_inc(s["cols_read"], 1)

            def exponents(la, b, par):
                n = la.done + b
                dve.wait_ge(s["dmax_ready"], n + 1)
                wait_for(dve, s["r_col_ready"], n - 1)
                nc.vector.tensor_scalar(drop[:, par, :], cols[:, par, :, 1], dmax[:, par:par + 1], None,
                                        ALU.subtract).then_inc(s["drop_ready"], 1)
                nc.vector.tensor_scalar(top[:, par, :], cols[:, par, :, 0], dmax[:, par:par + 1], T_MAX, ALU.add,
                                        ALU.min)
                dve.wait_ge(s["drop_ready"], n + 1)
                nc.vector.tensor_scalar(rise[:, par, :], drop[:, par, :], -RISE, Q_MAX, ALU.mult,
                                        ALU.min).then_inc(s["args_ready"], 1)

            def tile(la, b, par, k):
                n = la.done + b
                if k == 0:
                    dve.wait_ge(s["q_ready"], n + 1)
                    dve.wait_ge(s["r_ready"], n + 1)
                wait_for(dve, s["tile_used"], T * n + k - RING + 1)
                nc.vector.scalar_tensor_tensor(tiles[:, k % RING, :], r_row[:, par, :], q[:, par, k:k + 1],
                                               la.mask[:, k, :], ALU.max, ALU.mult).then_inc(s["tile_ready"], 1)

            def finish(la, b, par):
                n = la.done + b
                if la.elu:
                    dve.wait_ge(s["empty_ready"], n + 1)
                else:
                    dve.wait_ge(s["addend_ready"], la.addends + b + 1)
                for bank in range(BANKS):
                    if bank < BANKS - 1:
                        dve.wait_ge(s["bank_done"], (BANKS - 1) * n + bank + 1)
                    else:
                        dve.wait_ge(s["tile_used"], T * (n + 1))
                    lo, hi = 3 * bank, min(3 * bank + 3, T)
                    sums = ps[:, bank, 0:(hi - lo) * V1].rearrange("p (t c) -> p t c", c=V1)[:, :, D]
                    nc.vector.tensor_tensor(den[:, lo:hi], sums, la.empty[:, lo:hi],
                                            ALU.add).then_inc(s["den_ready"], 1)
                    dve.wait_ge(s["den_ready"], BANKS * n + bank + 1)
                    nc.vector.reciprocal(recip[:, lo:hi], den[:, lo:hi]).then_inc(s["recip_ready"], 1)
                    dve.wait_ge(s["recip_ready"], BANKS * n + bank + 1)
                    for it in range(lo, hi):
                        dst = y[:, it, :] if la.elu else g.x[:, b, it, :]
                        last = nc.vector.scalar_tensor_tensor(dst, acc(it, 0, D), recip[:, it:it + 1],
                                                              addend[:, par, it, :], ALU.mult, ALU.add)
                    last.then_inc(s["acc_read"], 1)

            def elu_parts(la, b, par):
                if not la.elu:
                    return
                dve.wait_ge(s["acc_read"], BANKS * (la.done + b + 1))
                wait_for(dve, s["elu_exp"], b)
                nc.vector.tensor_scalar(low[:], y[:], 0.0, None, ALU.min)
                nc.vector.scalar_tensor_tensor(g.x[:, b], y[:], 0.0, g.x[:, b], ALU.max,
                                               ALU.add).then_inc(s["low_ready"], 1)

            def step(la, b, par):
                for k in range(T):
                    tile(la, b, par, k)
                    if k == 2:
                        begin(finish, -1)(la, b, par)
                    if k == 3:
                        begin(read_cols, 1)(la, b, par)
                    if k == 4:
                        norming(layer_moments, dve)(la, b, par)
                        begin(exponents, 1)(la, b, par)
                    if k == 5:
                        begin(elu_parts, -1)(la, b, par)

            layer_moments(nc, g, s, dve, first, 1)
            read_cols(first, 0, 0)
            exponents(first, 0, 0)
            steps(dve, step)
            finish(layers[-1], B - 1, 1)
            elu_parts(layers[-1], B - 1, 1)

        @block.scalar
        def _(act):
            def copy_ht(la, b, par):
                n = la.done + b
                act.wait_ge(s["turned"], n + 1)
                wait_for(act, s["v_done"], n - 1)
                nc.scalar.activation(halves(h_t[:, par, :]), turns, ACT.Copy,
                                     accum_out=h_sum[:, par:par + 1]).then_inc(s["ht_ready"], 1)

            def exps(la, b, par):
                n = la.done + b
                act.wait_ge(s["args_ready"], n + 1)
                wait_for(act, s["tile_used"], T * (n - 1))
                nc.scalar.activation(r_col[:, par, :], top[:, par, :], ACT.Exp, bias=g.bias_down[:],
                                     scale=RISE).then_inc(s["r_col_ready"], 1)
                nc.scalar.activation(q[:, par, :], rise[:, par, :], ACT.Exp,
                                     bias=g.bias_down[:]).then_inc(s["q_ready"], 1)
                nc.scalar.activation(v[:, par, :, D], drop[:, par, :], ACT.Exp,
                                     bias=g.bias_up[:]).then_inc(s["u_ready"], 1)

            def copy_row(la, b, par):
                n = la.done + b
                act.wait_ge(s["row_done"], n + 1)
                nc.scalar.activation(halves(r_row[:, par, :]), turns, ACT.Copy).then_inc(s["r_ready"], 1)

            def values(la, b, par):
                n = la.done + b
                act.wait_ge(s["v_done"], n + 1)
                act.wait_ge(s["u_ready"], n + 1)
                for jt in range(T):
                    last = nc.scalar.activation(v[:, par, jt, 0:D], val(jt, 0, D), ACT.Copy, scale=v[:, par, jt, D:V1])
                last.then_inc(s["v_ready"], 1)

            def elu_exp(la, b, par):
                if not la.elu:
                    return
                act.wait_ge(s["low_ready"], b + 1)
                wait_for(act, s["x_done"], b)
                nc.scalar.activation(ex[:], low[:], ACT.Exp).then_inc(s["elu_exp"], 1)

            def step(la, b, par):
                begin(exps, 1)(la, b, par)
                begin(copy_row, 1)(la, b, par)
                norming(layer_norm, act)(la, b, par)
                begin(values, 1)(la, b, par)
                begin(copy_ht, 2)(la, b, par)
                begin(elu_exp, -1)(la, b, par)

            copy_ht(first, 0, 0)
            layer_norm(nc, g, s, act, first, 1)
            exps(first, 0, 0)
            copy_row(first, 0, 0)
            values(first, 0, 0)
            copy_ht(first, 1, 1)
            steps(act, step)
            elu_exp(layers[-1], B - 1, 1)

        @block.gpsimd
        def _(pool):
            def reduce_max(la, b, par):
                n = la.done + b
                wait_alone(pool, g.pool_passed, s["cols_read"], n + 1)
                nc.gpsimd.partition_all_reduce(dmax[:, par:par + 1], dmax1[:], P,
                                               REDUCE_MAX).then_inc(s["dmax_ready"], 1)

            def make_addend(la, b, par):
                n = la.done + b
                wait_alone(pool, g.pool_passed, s["acc_read"], BANKS * (n - 1))
                dst = addend[:, par] if la.elu else spread[:]
                if not la.elu:
                    wait_alone(pool, g.pool_passed, s["addend_ready"], la.addends + b)
                last = nc.gpsimd.tensor_tensor(dst, la.empty[:].unsqueeze(2).to_broadcast([P, T, D]),
                                               mean_v[:, par:par + 1, :].to_broadcast([P, T, D]), ALU.mult)
                last.then_inc(s["empty_ready"], 1)
                if not la.elu:
                    if la.after_elu:
                        wait_alone(pool, g.pool_passed, s["x_done"], b + 1)
                    wait_alone(pool, g.pool_passed, s["empty_ready"], n + 1)
                    nc.gpsimd.tensor_tensor(addend[:, par], spread[:], g.x[:, b],
                                            ALU.add).then_inc(s["addend_ready"], 1)

            def elu_add(la, b, par):
                if not la.elu:
                    return
                wait_alone(pool, g.pool_passed, s["elu_exp"], b + 1)
                nc.gpsimd.tensor_scalar(ex[:], ex[:], -1.0, None, ALU.add).then_inc(s["elu_less"], 1)
                wait_alone(pool, g.pool_passed, s["elu_less"], b + 1)
                nc.gpsimd.tensor_tensor(g.x[:, b], g.x[:, b], ex[:], ALU.add).then_inc(s["x_done"], 1)

            def step(la, b, par):
                begin(reduce_max, 1)(la, b, par)
                norming(layer_inverse_root, pool)(la, b, par)
                begin(make_addend, 1)(la, b, par)
                begin(elu_add, -1)(la, b, par)

            layer_inverse_root(nc, g, s, pool, first, 1)
            reduce_max(first, 0, 0)
            make_addend(first, 0, 0)
            steps(pool, step)
            elu_add(layers[-1], B - 1, 1)

        @block.tensor
        def _(pe):
            def turn(la, b, par):
                n = la.done + b
                pe.wait_ge(s["h_ready"], la.normed + b + 1)
                wait_for(pe, s["r_ready"], n)
                for it in range(T):
                    last = nc.tensor.transpose(turns[:, it // 4, (it % 4) * P:(it % 4 + 1) * P], h[:, it, :],
                                               g.ident[:])
                last.then_inc(s["turned"], 1)

            def values(la, b, par):
                n = la.done + b
                pe.wait_ge(s["ht_ready"], n + 1)
                wait_for(pe, s["v_ready"], n)
                wait_for(pe, s["cols_read"], n)
                for jt in range(T):
                    nc.tensor.matmul(val(jt, 0, V2), h_t[:, par, jt * P:(jt + 1) * P], la.w, start=True, stop=True)
                nc.tensor.matmul(mean_ps, h_sum[:, par:par + 1].to_broadcast([P, P]), la.w[:, 0:D],
                                 start=True, stop=True).then_inc(s["v_done"], 1)

            def source_row(la, b, par):
                n = la.done + b
                pe.wait_ge(s["r_col_ready"], n + 1)
                pe.wait_ge(s["ht_ready"], n + 1)
                for it in range(T):
                    last = nc.tensor.transpose(turns[:, it // 4, (it % 4) * P:(it % 4 + 1) * P],
                                               r_col[:, par, it:it + 1].to_broadcast([P, P]), g.ident[:])
                last.then_inc(s["row_done"], 1)

            def products(la, b, par, k):
                n = la.done + b
                if k == 0:
                    pe.wait_ge(s["v_ready"], n + 1)
                pe.wait_ge(s["tile_ready"], T * n + k + 1)
                for it in range(T):
                    new_bank = k == 0 and it % 3 == 0
                    if new_bank:
                        wait_for(pe, s["acc_read"], BANKS * (n - 1) + it // 3 + 1)
                    last = nc.tensor.matmul(acc(it, 0, V1), tiles[:, k % RING, it * P:(it + 1) * P], v[:, par, k, :],
                                            start=new_bank, stop=(k == T - 1), skip_group_check=True)
                    if k == T - 1 and it % 3 == 2:
                        last.then_inc(s["bank_done"], 1)
                last.then_inc(s["tile_used"], 1)

            def step(la, b, par):
                for k in range(T):
                    products(la, b, par, k)
                    if k == 3:
                        begin(source_row, 1)(la, b, par)
                    if k == 6:
                        begin(turn, 2)(la, b, par)
                    if k == 7:
                        begin(values, 2)(la, b, par)

            turn(first, 0, 0)
            values(first, 0, 0)
            source_row(first, 0, 0)
            turn(first, 1, 1)
            values(first, 1, 1)
            steps(pe, step)

        if out_h is not None:
            last_layer = layers[-1]

            @block.sync
            def _(sp):
                out_v = out_h.rearrange("b (t p) d -> p b t d", p=P)
                with sp.Fori(0, B) as b:
                    sp.wait_ge(s["acc_read"], BANKS * (last_layer.done + b + 1))
                    sp.dma_start(out_v[:, b], g.x[:, b]).then_inc(out_done, 16)
                sp.wait_ge(out_done, 16 * B)


def head_layer(nc, g, s, next_layer):
    with ExitStack() as ctx:
        def sb(name, shape, dt=FP32):
            return ctx.enter_context(nc.sbuf_tensor(name + "_l1", shape, dt))

        def sem(name):
            return ctx.enter_context(nc.semaphore("h_" + name))

        mask_off = sb("mask_off", [P, T, N], BF16)
        stats, mom, var_eps, rstd = g.stats, g.mom, g.var_eps, g.rstd
        hn = g.h
        h_rest = sb("h_rest", [P, T, D])
        h_part = sb("h_part", [P, 3, T, D], BF16)
        h_t = sb("h_t", [P, N])
        off_t = sb("off_t", [P, N])
        row_rest = h_rest[0:2 * H].rearrange("p t d -> p (t d)")
        row_mid = hn[0:2 * H, 0:T // 2, :].rearrange("p t d -> p (t d)").bitcast(BF16)
        row_part = sb("row_part", [96, N], BF16)
        cols = sb("cols", [P, T, 2, H])
        dmax1, dmax, clamp = sb("dmax1", [P, H]), sb("dmax", [P, H]), sb("clamp", [P, H])
        top = sb("top", [P, T, H])
        args = sb("args", [P, 3, T, H])
        U, Q, R, MINUS_Q, C = range(5)
        batch_cols = sb("batch_cols", [P, 5, T, H])
        head_cols = sb("head_cols", [P, 2, 5, T])
        weights = sb("weights", [P, 2, T, H])
        weight_part = sb("weight_part", [P, T, H, 2, 3], BF16)
        head_part = sb("head_part", [P, 2, T, 2, 3], BF16)
        r_row = sb("r_row", [P, 2, N])
        v = sb("v", [P, 2, T, D])
        off = sb("off", [P, 2, T, D])
        tiles = sb("tiles", [P, RING, N])
        sign = sb("sign", [P, T, N], BF16)
        sums, totals, total = sb("sums", [P, T, 2]), sb("totals", [P, H, 2]), sb("total", [P, 2])
        high, minus_den = sb("high", [P, T]), sb("minus_den", [P, T])
        recip, scale = sb("recip", [P, T]), sb("scale", [P, T])
        ones = sb("ones", [P, P], BF16)
        z = sb("z", [P, 2, T, D])

        ps = ctx.enter_context(nc.psum_tensor("ps_l1", [P, 8, HALF], FP32))
        aux_a, aux_b = ps[:, 4:6, :], ps[:, 6, :]
        sums_ps = ps[:, 7, 0:T * 6]
        totals_ps = ps[:, 7, T * 6:(T + H) * 6]

        stats_done, moments_done, var_ready, rstd_done, normed = (
            sem("stats"), sem("moments"), sem("var_ready"), sem("rstd"), sem("normed"))
        turned, h_ready, cols_done, cols_read, dmax_ready = (
            sem("turned"), sem("h_ready"), sem("cols_done"), sem("cols_read"), sem("dmax_ready"))
        top_ready, half_args, args_ready, exps_ready = sem("top"), sem("half_args"), sem("args"), sem("exps")
        weights_ready, high_part, weights_rest, mid_part, cols_ready = (
            sem("weights_ready"), sem("high_part"), sem("weights_rest"), sem("mid_part"), sem("cols_ready"))
        rows_done, hi_ready, rest_ready, mid_ready, mid_moved, rows_ready = (
            sem("rows_done"), sem("hi_ready"), sem("rest_ready"), sem("mid_ready"), sem("mid_moved"), sem("rows_ready"))
        relu_ready, rest1, part1, parts_ready = sem("relu_ready"), sem("rest1"), sem("part1"), sem("parts_ready")
        off_done, off_ready = sem("off_done"), sem("off_ready")
        off_mask_ready, ones_ready, part_zero = sem("off_mask_ready"), sem("ones_ready"), sem("part_zero")
        base_added = sem("base_added")
        head_ready, src_done, src_read, r_ready, v_done, v_ready = (
            sem("head_ready"), sem("src_done"), sem("src_read"), sem("r_ready"), sem("v_done"), sem("v_ready"))
        offv_done, offv_read = sem("offv_done"), sem("offv_read")
        totals_read = sem("totals_read")
        sums_read, high_ready, den_ready = sem("sums_read"), sem("high_ready"), sem("den_ready")
        recip_ready, scale_ready, z_ready, tanh_ready, weighed, x_done = (
            sem("recip_ready"), sem("scale_ready"), sem("z_ready"), sem("tanh_ready"), sem("weighed"), sem("x_done"))
        tile_ready, tile_used, sign_ready, sign_used = (
            sem("tile_ready"), sem("tile_used"), sem("sign_ready"), sem("sign_used"))

        block = ctx.enter_context(nc.Block())

        def all_maps(eng, step):
            def pair(b, h, first=False, last=False, shared=False):
                step(b, h, 0, first=first, shared=shared)
                step(b, h + 1, 1, last=last, shared=shared)

            pair(0, 0, first=True)
            with eng.Fori(0, B - 1) as b:
                with eng.Fori(1, H // 2 - 1) as hp:
                    pair(b, 2 * hp)
                pair(b, H - 2, shared=True)
                pair(b + 1, 0)
            with eng.Fori(1, H // 2 - 1) as hp:
                pair(B - 1, 2 * hp)
            pair(B - 1, H - 2, last=True)

        def following(b, h):
            return (b + 1, 0) if isinstance(h, int) and h == H - 1 else (b, h + 1)

        def before(b, h):
            return (b - 1, H - 1) if isinstance(h, int) and h == 0 else (b, h - 1)

        def split_h(ns, eng, passed, b):
            wait_alone(eng, passed, normed, b)
            wait_alone(eng, passed, off_done, 2 * b)
            wait_alone(eng, passed, rows_ready, b)
            ns.tensor_scalar(h_part[:, 0], hn[:], 0.0, None, ALU.max)
            ns.tensor_scalar(h_rest[:], hn[:], 0.0, None, ALU.max).then_inc(relu_ready, 1)
            wait_alone(eng, passed, relu_ready, b + 1)
            ns.tensor_tensor(h_rest[:], h_rest[:], h_part[:, 0], ALU.subtract).then_inc(rest1, 1)
            wait_alone(eng, passed, rest1, b + 1)
            ns.tensor_copy(h_part[:, 1], h_rest[:]).then_inc(part1, 1)
            wait_alone(eng, passed, part1, b + 1)
            ns.tensor_tensor(h_part[:, 2], h_rest[:], h_part[:, 1], ALU.subtract).then_inc(parts_ready, 1)

        @block.vector
        def _(dve):
            def moments(b):
                for it in range(T):
                    last = nc.vector.bn_stats(stats[:, it, :], g.x[:, b, it, :])
                last.then_inc(stats_done, 1)
                wait_alone(dve, g.dve_passed, stats_done, b)
                for it in range(T):
                    last = nc.vector.bn_aggr(mom[:, it, :], stats[:, it, :])
                last.then_inc(moments_done, 1)
                dve.wait_ge(moments_done, b)
                nc.vector.tensor_scalar(var_eps[:], mom[:, :, 1], EPS, None, ALU.add).then_inc(var_ready, 1)

            def norm(b):
                wait_for(dve, turned, b)
                wait_for(dve, relu_ready, b)
                wait_for(dve, mid_moved, b)
                dve.wait_ge(rstd_done, b)
                for it in range(T):
                    last = nc.vector.tensor_scalar(hn[:, it, :], g.x[:, b, it, :], mom[:, it, 0:1],
                                                   rstd[:, it:it + 1], ALU.subtract, ALU.mult)
                last.then_inc(normed, 1)

            def read_cols(b):
                dve.wait_ge(cols_done, b + 1)
                nc.vector.tensor_reduce(dmax1[:], aux_b[:, 0:2 * T * H].rearrange(
                    "p (t c h) -> p c h t", t=T, c=2)[:, 1, :, :], AX_X, ALU.max)
                nc.vector.tensor_copy(cols[:].rearrange("p t c h -> p (t c h)"),
                                      aux_b[:, 0:2 * T * H]).then_inc(cols_read, 1)

            def exponents(b):
                dve.wait_ge(dmax_ready, b + 1)
                dve.wait_ge(cols_read, b + 1)
                over_tiles = dmax[:].unsqueeze(1).to_broadcast([P, T, H])
                nc.vector.tensor_tensor(top[:], cols[:, :, 0, :], over_tiles, ALU.add)
                nc.vector.tensor_scalar(clamp[:], dmax[:], -1.0, T_MAX, ALU.mult, ALU.add)
                nc.vector.tensor_tensor(args[:, 0], cols[:, :, 1, :], over_tiles, ALU.subtract).then_inc(top_ready, 1)
                dve.wait_ge(top_ready, b + 1)
                nc.vector.tensor_copy(batch_cols[:, C], clamp[:].unsqueeze(1).to_broadcast([P, T, H]))
                nc.vector.tensor_scalar(args[:, 1], args[:, 0], -RISE, Q_MAX, ALU.mult, ALU.min)
                nc.vector.tensor_scalar(args[:, 2], top[:], T_MAX, RISE, ALU.min, ALU.mult).then_inc(half_args, 1)
                dve.wait_ge(half_args, b + 1)
                nc.vector.tensor_scalar(args[:, 0], args[:, 0], SHIFT, None, ALU.add)
                nc.vector.tensor_scalar(args[:, 1:3], args[:, 1:3], -SHIFT, None, ALU.add).then_inc(args_ready, 1)

            def split_weights(b):
                dve.wait_ge(exps_ready, b + 1)
                nc.vector.tensor_scalar(batch_cols[:, MINUS_Q], batch_cols[:, Q], -1.0, None, ALU.mult)
                nc.vector.tensor_copy(weights[:, 0], batch_cols[:, U])
                nc.vector.tensor_tensor(weights[:, 1], batch_cols[:, U], batch_cols[:, Q],
                                        ALU.mult).then_inc(weights_ready, 1)
                dve.wait_ge(weights_ready, b + 1)
                part = weight_part[:].rearrange("p t h c w -> p c (t h) w")
                left = weights[:].rearrange("p c t h -> p c (t h)")
                nc.vector.tensor_copy(part[:, :, :, 0], left).then_inc(high_part, 1)
                dve.wait_ge(high_part, b + 1)
                nc.vector.tensor_tensor(left, left, part[:, :, :, 0], ALU.subtract).then_inc(weights_rest, 1)
                dve.wait_ge(weights_rest, b + 1)
                nc.vector.tensor_copy(part[:, :, :, 1], left).then_inc(mid_part, 1)
                dve.wait_ge(mid_part, b + 1)
                nc.vector.tensor_tensor(part[:, :, :, 2], left, part[:, :, :, 1], ALU.subtract).then_inc(cols_ready, 1)

            def split_rows(b):
                dve.wait_ge(rows_done, b + 1)
                dve.wait_ge(parts_ready, b + 1)
                dve.wait_ge(turned, b + 1)
                wait_for(dve, src_done, 2 * H * b)
                if isinstance(b, int) and b == 0:
                    dve.wait_ge(part_zero, 1)
                rows = aux_a[0:2 * H]
                hi = row_part[0:2 * H, :].rearrange("p (a n) -> p a n", a=2)
                nc.vector.tensor_copy(hi, rows).then_inc(hi_ready, 1)
                dve.wait_ge(hi_ready, b + 1)
                nc.vector.tensor_tensor(row_rest.rearrange("p (a n) -> p a n", a=2), rows, hi,
                                        ALU.subtract).then_inc(rest_ready, 1)
                dve.wait_ge(rest_ready, b + 1)
                nc.vector.tensor_copy(row_mid, row_rest).then_inc(mid_ready, 1)
                dve.wait_ge(mid_ready, b + 1)
                nc.vector.tensor_tensor(row_part[64:64 + 2 * H, :], row_rest, row_mid,
                                        ALU.subtract).then_inc(rows_ready, 1)

            def take_head(b, h, par):
                m = H * b + h
                dve.wait_ge(cols_ready, b + 1)
                wait_for(dve, sign_used, T * (m - 1))
                nc.vector.tensor_copy(head_part[:, par], weight_part[:, :, bass.ds(h, 1)]
                                      .rearrange("p t o c w -> p t (o c) w"))
                nc.vector.tensor_copy(head_cols[:, par], batch_cols[:, :, :, bass.ds(h, 1)]
                                      .rearrange("p c t o -> p c (t o)")).then_inc(head_ready, 1)

            def values(b, h, par):
                m = H * b + h
                dve.wait_ge(v_done, m + 1)
                dve.wait_ge(head_ready, m + 1)
                for half in range(2):
                    ts = slice(4 * half, 4 * half + 4)
                    last = nc.vector.tensor_tensor(
                        v[:, par, ts, :], aux_a[:, half, :].rearrange("p (t d) -> p t d", d=D),
                        head_cols[:, par, U, ts].unsqueeze(2).to_broadcast([P, 4, D]), ALU.mult)
                last.then_inc(v_ready, 1)

            def tile(m, par, k):
                if k == 0:
                    dve.wait_ge(r_ready, m + 1)
                wait_for(dve, tile_used, T * m + k - RING + 1)
                nc.vector.scalar_tensor_tensor(tiles[:, k % RING, :], r_row[:, par, :], head_cols[:, par, Q, k:k + 1],
                                               g.mask_gt[:, k, :], ALU.max, ALU.mult).then_inc(tile_ready, 1)

            def finish(b, h, par):
                m = H * b + h
                dve.wait_ge(sign_used, T * (m + 1))
                if isinstance(h, int) and h == 0:
                    nc.vector.tensor_reduce(totals[:].rearrange("p h c -> p (h c)"),
                                            totals_ps.rearrange("p (t w) -> p t w", w=3), AX_X,
                                            ALU.add).then_inc(totals_read, 1)
                    dve.wait_ge(totals_read, b + 1)
                nc.vector.tensor_copy(total[:], totals[:, bass.ds(h, 1), :].rearrange("p o c -> p (o c)"))
                nc.vector.tensor_reduce(sums[:].rearrange("p t c -> p (t c)"),
                                        sums_ps.rearrange("p (t w) -> p t w", w=3), AX_X,
                                        ALU.add).then_inc(sums_read, 1)
                dve.wait_ge(sums_read, m + 1)
                nc.vector.scalar_tensor_tensor(high[:], sums[:, :, 0], total[:, 0:1], head_cols[:, par, R, :],
                                               ALU.add, ALU.mult).then_inc(high_ready, 1)
                dve.wait_ge(high_ready, m + 1)
                nc.vector.scalar_tensor_tensor(minus_den[:], sums[:, :, 1], total[:, 1:2], high[:],
                                               ALU.subtract, ALU.subtract).then_inc(den_ready, 1)
                dve.wait_ge(den_ready, m + 1)
                nc.vector.reciprocal(recip[:], minus_den[:]).then_inc(recip_ready, 1)
                dve.wait_ge(recip_ready, m + 1)
                nc.vector.tensor_scalar(scale[:], recip[:], -2.0, None, ALU.mult).then_inc(scale_ready, 1)
                dve.wait_ge(scale_ready, m + 1)
                dve.wait_ge(tile_used, T * (m + 1))
                dve.wait_ge(offv_read, m + 1)
                if not isinstance(m, int) or m >= 2:
                    dve.wait_ge(x_done, m)
                for it in range(T):
                    last = nc.vector.scalar_tensor_tensor(
                        z[:, par, it, :], ps[:, 2 * par + it // 4, (it % 4) * D:(it % 4 + 1) * D],
                        scale[:, it:it + 1], off[:, par, it, :], ALU.mult, ALU.add)
                last.then_inc(z_ready, 1)

            def step(b, h, par, first=False, last=False, shared=False):
                m = H * b + h
                b1, h1 = following(b, h)
                for k in range(T):
                    tile(m, par, k)
                    if k == 0 and shared and par == 0:
                        moments(b + 1)
                    if k == 1 and shared and par == 0:
                        norm(b + 1)
                    if k == 1 and last:
                        dve.wait_ge(x_done, H + 1)
                        layer_moments(nc, g, s, dve, next_layer, 0)
                    if k == 2 and shared and par == 1:
                        read_cols(b + 1)
                    if k == 3:
                        if not first:
                            finish(*before(b, h), 1 - par)
                        if shared and par == 1:
                            exponents(b + 1)
                        elif not last:
                            take_head(b1, h1, 1 - par)
                    if k == 4 and shared and par == 1:
                        split_rows(b + 1)
                    if k == 5 and shared and par == 1:
                        split_weights(b + 1)
                        take_head(b1, h1, 1 - par)
                    if k == (7 if shared and par == 1 else 5) and not last:
                        values(b1, h1, 1 - par)

            split_h(nc.vector, dve, g.dve_passed, 0)
            nc.vector.tensor_scalar(mask_off[:], g.mask_gt[:], -1.0, 1.0, ALU.mult, ALU.add).then_inc(off_mask_ready, 1)
            read_cols(0)
            exponents(0)
            split_rows(0)
            split_weights(0)
            take_head(0, 0, 0)
            values(0, 0, 0)
            all_maps(dve, step)
            finish(B - 1, H - 1, 1)

        @block.scalar
        def _(act):
            def relu_h(b):
                act.wait_ge(turned, b + 1)
                wait_for(act, v_done, H * b)
                nc.scalar.activation(h_t[:].rearrange("p (a n) -> p a n", a=2), aux_a, ACT.Relu).then_inc(h_ready, 1)

            def exps(b):
                act.wait_ge(args_ready, b + 1)
                wait_for(act, head_ready, H * b)
                nc.scalar.activation(batch_cols[:, U:R + 1], args[:], ACT.Exp).then_inc(exps_ready, 1)

            def move_mid(b):
                act.wait_ge(mid_ready, b + 1)
                wait_for(act, src_done, 2 * H * b)
                if isinstance(b, int) and b == 0:
                    act.wait_ge(part_zero, 1)
                nc.scalar.activation(row_part[32:32 + 2 * H, :], row_mid, ACT.Copy).then_inc(mid_moved, 1)

            def off_rows(b, half):
                act.wait_ge(off_done, 2 * b + half + 1)
                wait_for(act, offv_done, H * b)
                nc.scalar.activation(off_t[:, half * HALF:(half + 1) * HALF], aux_b, ACT.Copy,
                                     scale=NEG_BIG).then_inc(off_ready, 1)

            def source(m, par, half):
                act.wait_ge(head_ready, m + 1)
                act.wait_ge(src_done, 2 * m + half + 1)
                wait_for(act, tile_ready, T * (m - 1))
                nc.scalar.activation(r_row[:, par, half * HALF:(half + 1) * HALF], aux_b, ACT.Relu,
                                     bias=head_cols[:, par, C, 0:1], scale=-1.0).then_inc(src_read, 1)

            def r_exp(m, par):
                act.wait_ge(src_read, 2 * m + 2)
                nc.scalar.activation(r_row[:, par, :], r_row[:, par, :], ACT.Exp, bias=g.bias_r[:],
                                     scale=-RISE).then_inc(r_ready, 1)

            def off_values(m, par):
                act.wait_ge(offv_done, m + 1)
                wait_for(act, z_ready, m - 1)
                nc.scalar.activation(off[:, par].rearrange("p (a t) d -> p a (t d)", a=2), aux_a,
                                     ACT.Copy).then_inc(offv_read, 1)

            def signs(m, par, k):
                if k == 0:
                    act.wait_ge(r_ready, m + 1)
                wait_for(act, sign_used, T * (m - 1) + k + 1)
                nc.scalar.activation(sign[:, k, :], r_row[:, par, :], ACT.Sign,
                                     bias=head_cols[:, par, MINUS_Q, k:k + 1]).then_inc(sign_ready, 1)

            def tanh(m, par):
                act.wait_ge(z_ready, m + 1)
                nc.scalar.activation(z[:, par], z[:, par], ACT.Tanh, scale=0.5).then_inc(tanh_ready, 1)

            def step(b, h, par, first=False, last=False, shared=False):
                m = H * b + h
                last_head = shared and par == 1
                for k in range(T):
                    signs(m, par, k)
                    if last_head:
                        if k == 1:
                            off_rows(b + 1, 0)
                        if k == 2:
                            exps(b + 1)
                        if k == 3:
                            off_rows(b + 1, 1)
                            move_mid(b + 1)
                    if not last:
                        if k == (5 if last_head else 2):
                            source(m + 1, 1 - par, 0)
                        if k == (6 if last_head else 3):
                            source(m + 1, 1 - par, 1)
                            r_exp(m + 1, 1 - par)
                        if k == (7 if last_head else 5):
                            off_values(m + 1, 1 - par)
                    if k == (7 if last_head else 4) and not first:
                        tanh(m - 1, 1 - par)
                if shared and par == 0:
                    relu_h(b + 1)
                if last:
                    act.wait_ge(turned, B)
                    act.wait_ge(relu_ready, B)
                    act.wait_ge(rows_ready, B)
                    layer_norm(nc, g, s, act, next_layer, 0)

            relu_h(0)
            exps(0)
            move_mid(0)
            off_rows(0, 0)
            off_rows(0, 1)
            source(0, 0, 0)
            source(0, 0, 1)
            r_exp(0, 0)
            off_values(0, 0)
            all_maps(act, step)
            tanh(B * H - 1, 1)

        @block.gpsimd
        def _(pool):
            def add_base(b):
                nc.gpsimd.tensor_tensor(g.x[:, b], g.x[:, b], g.base1[:].unsqueeze(2).to_broadcast([P, T, D]),
                                        ALU.add).then_inc(base_added, 1)

            def inverse_root(b):
                wait_alone(pool, g.pool_passed, var_ready, b)
                nc.gpsimd.tensor_tensor(rstd[:], var_eps[:], g.minus_half[:], ALU.pow).then_inc(rstd_done, 1)

            def reduce_max(b):
                wait_alone(pool, g.pool_passed, cols_read, b + 1)
                nc.gpsimd.partition_all_reduce(dmax[:], dmax1[:], P, REDUCE_MAX).then_inc(dmax_ready, 1)

            def weigh(b, h, m, par):
                wait_alone(pool, g.pool_passed, tanh_ready, m + 1)
                nc.gpsimd.tensor_tensor(z[:, par], z[:, par],
                                        g.half_w[:, bass.ds(h, 1)].unsqueeze(2).to_broadcast([P, T, D]),
                                        ALU.mult).then_inc(weighed, 1)
                wait_alone(pool, g.pool_passed, weighed, m + 1)
                wait_alone(pool, g.pool_passed, base_added, b + 1)
                wait_alone(pool, g.pool_passed, x_done, m + 1)
                nc.gpsimd.tensor_tensor(g.x[:, b], g.x[:, b], z[:, par], ALU.add).then_inc(x_done, 1)

            def step(b, h, par, first=False, last=False, shared=False):
                m = H * b + h
                if shared and par == 0:
                    inverse_root(b + 1)
                    split_h(nc.gpsimd, pool, g.pool_passed, b + 1)
                if last:
                    layer_inverse_root(nc, g, s, pool, next_layer, 0)
                if not first:
                    weigh(*before(b, h), m - 1, 1 - par)
                if shared and par == 0:
                    add_base(b + 1)
                    reduce_max(b + 1)

            nc.gpsimd.memset(row_part[:], 0.0).then_inc(part_zero, 1)
            nc.gpsimd.memset(ones[:], 1.0).then_inc(ones_ready, 1)
            pool.sem_inc(x_done, 1)
            add_base(0)
            reduce_max(0)
            all_maps(pool, step)
            weigh(B - 1, H - 1, B * H - 1, 1)

        @block.tensor
        def _(pe):
            def turn(b):
                wait_for(pe, normed, b)
                wait_for(pe, offv_read, H * b)
                for it in range(T):
                    last = nc.tensor.transpose(aux_a[:, it // 4, (it % 4) * P:(it % 4 + 1) * P], hn[:, it, :],
                                               g.ident[:])
                last.then_inc(turned, 1)

            def score_cols(b):
                pe.wait_ge(h_ready, b + 1)
                wait_for(pe, src_read, 2 * H * b)
                for jt in range(T):
                    last = nc.tensor.matmul(aux_b[:, 2 * H * jt:2 * H * (jt + 1)], h_t[:, jt * P:(jt + 1) * P],
                                            g.wa_heads[:].rearrange("p c h -> p (c h)"), start=True, stop=True)
                last.then_inc(cols_done, 1)

            def score_rows(b):
                pe.wait_ge(h_ready, b + 1)
                for half in range(2):
                    last = nc.tensor.matmul(aux_a[0:2 * H, half, :], g.wa_heads[:].rearrange("p c h -> p (c h)"),
                                            h_t[:, half * HALF:(half + 1) * HALF], start=True, stop=True)
                last.then_inc(rows_done, 1)

            def off_sums(b, half):
                if half == 0:
                    pe.wait_ge(parts_ready, b + 1)
                    pe.wait_ge(off_mask_ready, 1)
                    pe.wait_ge(cols_read, b + 1)
                else:
                    pe.wait_ge(off_ready, 2 * b + 1)
                for jt in range(T):
                    for part in range(3):
                        last = nc.tensor.matmul(aux_b, h_part[:, part, jt, :],
                                                mask_off[:, jt, half * HALF:(half + 1) * HALF],
                                                start=(jt == 0 and part == 0), stop=(jt == T - 1 and part == 2))
                last.then_inc(off_done, 1)

            def source(b, h, m, half, new_batch):
                if half == 1:
                    pe.wait_ge(src_read, 2 * m + 1)
                elif new_batch:
                    pe.wait_ge(off_ready, 2 * b + 2)
                    pe.wait_ge(rows_ready, b + 1)
                    pe.wait_ge(mid_moved, b + 1)
                else:
                    pe.wait_ge(src_read, 2 * m)
                nc.tensor.matmul(aux_b, g.sel[0:96, bass.ds(h, 1), :].rearrange("k o p -> k (o p)"),
                                 row_part[:, half * HALF:(half + 1) * HALF], start=True,
                                 stop=True).then_inc(src_done, 1)

            def values(b, h, m, new_batch):
                if new_batch:
                    pe.wait_ge(rest_ready, b + 1)
                else:
                    pe.wait_ge(offv_read, m)
                wh = g.w_heads[:, bass.ds(h, 1), :].rearrange("p o d -> p (o d)")
                for jt in range(T):
                    last = nc.tensor.matmul(aux_a[:, jt // 4, (jt % 4) * D:(jt % 4 + 1) * D],
                                            h_t[:, jt * P:(jt + 1) * P], wh, start=True, stop=True)
                last.then_inc(v_done, 1)

            def off_values(b, h, m):
                pe.wait_ge(v_ready, m + 1)
                wh = g.w_heads[:, bass.ds(h, 1), :].rearrange("p o d -> p (o d)")
                for it in range(T):
                    last = nc.tensor.matmul(aux_a[:, it // 4, (it % 4) * D:(it % 4 + 1) * D],
                                            off_t[:, it * P:(it + 1) * P], wh, start=True, stop=True)
                last.then_inc(offv_done, 1)

            def sign_sums(h, m, par, k):
                new_batch = isinstance(h, int) and h == 0
                if k == 0:
                    pe.wait_ge(head_ready, m + 1)
                    wait_for(pe, sums_read, m)
                    if new_batch:
                        if isinstance(m, int) and m == 0:
                            pe.wait_ge(ones_ready, 1)
                        for jt in range(T):
                            nc.tensor.matmul(totals_ps, ones[:], weight_part[:, jt].rearrange("p h c w -> p (h c w)"),
                                             start=(jt == 0), stop=(jt == T - 1), skip_group_check=True)
                pe.wait_ge(sign_ready, T * m + k + 1)
                for it in range(T):
                    last = nc.tensor.matmul(sums_ps[:, 6 * it:6 * it + 6], sign[:, k, it * P:(it + 1) * P],
                                            head_part[:, par, k].rearrange("p c w -> p (c w)"),
                                            start=(k == 0 and it == 0 and not new_batch), stop=(k == T - 1),
                                            skip_group_check=True)
                last.then_inc(sign_used, 1)

            def products(m, par, k):
                if k == 0:
                    pe.wait_ge(v_ready, m + 1)
                    wait_for(pe, z_ready, m - 1)
                pe.wait_ge(tile_ready, T * m + k + 1)
                for it in range(T):
                    last = nc.tensor.matmul(ps[:, 2 * par + it // 4, (it % 4) * D:(it % 4 + 1) * D],
                                            tiles[:, k % RING, it * P:(it + 1) * P], v[:, par, k, :],
                                            start=(k == 0 and it % 4 == 0), stop=(k == T - 1), skip_group_check=True)
                last.then_inc(tile_used, 1)

            def step(b, h, par, first=False, last=False, shared=False):
                m = H * b + h
                b1, h1 = following(b, h)
                last_head = shared and par == 1
                for k in range(T):
                    products(m, par, k)
                    if last_head:
                        if k == 0:
                            score_rows(b + 1)
                        if k == 1:
                            off_sums(b + 1, 0)
                        if k == 2:
                            off_sums(b + 1, 1)
                    if not last:
                        if k == (5 if last_head else 2):
                            source(b1, h1, m + 1, 0, last_head)
                            values(b1, h1, m + 1, last_head)
                        if k == (6 if last_head else 3):
                            source(b1, h1, m + 1, 1, last_head)
                        if k == (7 if last_head else 4):
                            off_values(b1, h1, m + 1)
                    if k % 4 == 3:
                        for j in range(k - 3, k + 1):
                            sign_sums(h, m, par, j)
                    if shared and par == 0:
                        if k == 6:
                            turn(b + 1)
                        if k == 7:
                            score_cols(b + 1)

            turn(0)
            score_cols(0)
            score_rows(0)
            off_sums(0, 0)
            off_sums(0, 1)
            source(0, 0, 0, 0, True)
            source(0, 0, 0, 1, True)
            values(0, 0, 0, True)
            off_values(0, 0, 0)
            all_maps(pe, step)


def gat_stack(nc, x_h, adj_h, w_in_h, w_out_h, a_h, avg_w_h, avg_b_h, out_h):
    with ExitStack() as ctx:
        def sb(name, shape, dt=FP32):
            return ctx.enter_context(nc.sbuf_tensor(name, shape, dt))

        g = Shared()
        g.x = sb("x_all", [P, B, T, D])
        g.mask_gt = sb("mask_gt", [P, T, N], BF16)
        g.mask_ne = sb("mask_ne", [P, T, N], UINT8)
        g.w_wide = sb("w_wide", [P, W_HEADS, D + 2])
        g.w_heads = sb("w_heads", [P, H, D])
        g.wa_heads = sb("wa_heads", [P, 2, H])
        g.ident = sb("ident", [P, P])
        g.sel = sb("sel", [P, H, P], BF16)
        g.empty_gt, g.empty_ne = sb("empty_gt", [P, T]), sb("empty_ne", [P, T])
        g.avg_w, g.avg_b = sb("avg_w", [P, H]), sb("avg_b", [P, 1])
        g.half_w, g.half_sum, g.base1 = sb("half_w", [P, H]), sb("half_sum", [P, 1]), sb("base1", [P, 1])
        g.minus_half = sb("minus_half", [P, T])
        g.stats, g.mom = sb("stats", [P, T, 6]), sb("mom", [P, T, 2])
        g.var_eps, g.rstd = sb("var_eps", [P, T]), sb("rstd", [P, T])
        g.minus_mean, g.shift = sb("minus_mean", [P, T]), sb("shift", [P, T])
        g.h = sb("h", [P, T, D])
        g.bias_up, g.bias_down, g.bias_r = sb("bias_up", [P, 1]), sb("bias_down", [P, 1]), sb("bias_r", [P, 1])

        g.pool_passed = ctx.enter_context(nc.semaphore("pool_passed"))
        g.dve_passed = ctx.enter_context(nc.semaphore("dve_passed"))
        g.x_in = [ctx.enter_context(nc.semaphore(f"x_in{i}")) for i in range(3)]

        s = masked_semaphores(nc, ctx)
        layer0, layer1, layer2, layer3 = (MaskedLayer(g, 0, 0), HeadLayer(), MaskedLayer(g, 2, 1),
                                          MaskedLayer(g, 3, 2))
        setup(nc, g, s, layer0, (x_h, adj_h, w_in_h, w_out_h, a_h, avg_w_h, avg_b_h))
        masked_layers(nc, g, s, [layer0], layer1, None)
        head_layer(nc, g, s, layer2)
        masked_layers(nc, g, s, [layer2, layer3], None, out_h)


def kernel(x, adj, L0_gnn_W, L0_gnn_a, L1_gnn_W, L1_gnn_a, L1_gnn_avg_w, L1_gnn_avg_b, L2_gnn_W, L2_gnn_a,
           L3_gnn_W, L3_gnn_a):
    import numpy as np
    import concourse.bacc as bacc
    from concourse.bass_utils import run_bass_kernel_spmd

    w0, w1, w2, w3 = (np.asarray(w) for w in (L0_gnn_W, L1_gnn_W, L2_gnn_W, L3_gnn_W))
    w_in = np.concatenate([w0[:, None], w2.T[:, None], w3.T[:, None], w1.transpose(1, 0, 2)], axis=1)
    w_out = np.concatenate([w0.T[:, None], w2[:, None], w3[:, None], w1.transpose(2, 0, 1)], axis=1)
    a = np.stack([np.asarray(v).reshape(2, 128).T for v in (L0_gnn_a, L2_gnn_a, L3_gnn_a)]
                 + [np.asarray(L1_gnn_a)[h].reshape(2, 128).T for h in range(8)], axis=1)
    arrays = {
        "x_in": np.asarray(x), "adj_in": np.asarray(adj), "w_in_in": w_in, "w_out_in": w_out, "a_in": a,
        "avg_w_in": np.broadcast_to(np.asarray(L1_gnn_avg_w).reshape(1, 8), (128, 8)),
        "avg_b_in": np.broadcast_to(np.asarray(L1_gnn_avg_b).reshape(1, 1), (128, 1)),
    }
    arrays = {k: np.ascontiguousarray(v) for k, v in arrays.items()}
    nc = bacc.Bacc("TRN2", target_bir_lowering=False, num_devices=1)
    aps = [nc.dram_tensor(k, v.shape, mybir.dt.from_np(v.dtype), kind="ExternalInput").ap() for k, v in arrays.items()]
    out = nc.dram_tensor("out", (16, 1024, 128), FP32, kind="ExternalOutput").ap()
    gat_stack(nc, *aps, out)
    r = run_bass_kernel_spmd(nc, [arrays], core_ids=[0])
    return r.results[0]["out"]
```
